# Optimizing a Trainium2 kernel written in Bass

```python
import numpy as np
import jax
import jax.numpy as jnp

def _softmax(x, axis=-1):
    return jax.nn.softmax(x, axis=axis)

def _gelu(x):
    return jax.nn.gelu(x, approximate=True)

def _silu(x):
    return jax.nn.silu(x)

def _sigmoid(x):
    return jax.nn.sigmoid(x)

def _layernorm(x, axis=-1, eps=1e-05):
    m = jnp.mean(x, axis=axis, keepdims=True)
    v = jnp.var(x, axis=axis, keepdims=True)
    return (x - m) / jnp.sqrt(v + eps)

def _scatter_add(tgt, idx, src, axis=0):
    return tgt.at[idx].add(src)

def _segment_sum(src, seg, n):
    return jax.ops.segment_sum(src, seg, n)
kernel_name = 'mk_gnn_resnorm_d1_gnn_r8_ba2033'

def setup_inputs(seed: int=0):
    np.random.seed(seed)
    _w = jnp.asarray

    def _rec_inputs():
        import jax
        import jax.numpy as jnp
        _gk = jax.random.key(seed)
        x = -0.000202 + 1 * jax.random.normal(jax.random.fold_in(_gk, 1), (6250, 128), jnp.float32)
        _s = jax.random.randint(jax.random.fold_in(_gk, 2), (100000,), 0, 6250, jnp.int32)
        _d = jax.random.randint(jax.random.fold_in(_gk, 3), (100000,), 0, 6250, jnp.int32)
        _loop = jnp.arange(6250, dtype=jnp.int32)
        src = jnp.concatenate([_s, _d, _loop])
        dst = jnp.concatenate([_d, _s, _loop])
        _o = jnp.argsort(dst, stable=True)
        src = src[_o]
        dst = dst[_o]
        edge_type_8 = jax.random.randint(jax.random.fold_in(_gk, 12), (206250,), 0, 8, jnp.int32)
        return (x, src, dst, edge_type_8)
    x, src, dst, edge_type_8 = _rec_inputs()

    def _L0_gnn_setup():
        import jax, jax.numpy as jnp
        import numpy as np
        N_NODES = 6250
        N_EDGES = 80000
        D_FEAT = 128
        NUM_RELS = 8
        EPS = 0.0
        key = jax.random.key(seed)
        k_feat, k_w, k_et, k_src, k_dst = jax.random.split(key, 5)
        feat = jax.random.normal(k_feat, (N_NODES, D_FEAT), dtype=jnp.float32)
        W = jax.random.normal(k_w, (NUM_RELS, D_FEAT, D_FEAT), dtype=jnp.float32) * 0.05
        etypes = jax.random.randint(k_et, (N_EDGES,), 0, NUM_RELS, dtype=jnp.int32)
        src = jax.random.randint(k_src, (N_EDGES,), 0, N_NODES, dtype=jnp.int32)
        dst = jax.random.randint(k_dst, (N_EDGES,), 0, N_NODES, dtype=jnp.int32)
        return {'feat': feat, 'W': W, 'etypes': etypes, 'src': src, 'dst': dst}
    _L0_gnn_all = _L0_gnn_setup()
    _L0_gnn_in = {k: v for k, v in _L0_gnn_all.items() if k in ('W',)}
    del _L0_gnn_all
    return {'x': x, 'src': src, 'dst': dst, 'edge_type_8': edge_type_8, 'L0_gnn_W': _L0_gnn_in['W']}

def reference(x, src, dst, edge_type_8, L0_gnn_W):
    import jax
    import jax.numpy as jnp

    def _L0_gnn_ref(feat, W, etypes, src, dst):
        import jax, jax.numpy as jnp
        import numpy as np
        N_NODES = 6250
        N_EDGES = 80000
        D_FEAT = 128
        NUM_RELS = 8
        EPS = 0.0
        n_nodes = feat.shape[0]
        num_rels = W.shape[0]
        x = feat[src]
        m = jnp.zeros_like(x)
        for r in range(num_rels):
            mask = (etypes == r)[:, None]
            m = m + jnp.where(mask, x, 0.0) @ W[r]
        neigh = jax.ops.segment_sum(m, dst, num_segments=n_nodes)
        return (1.0 + EPS) * feat + neigh
    x = _layernorm(x + _L0_gnn_ref(x, L0_gnn_W, edge_type_8, src, dst), axis=-1)
    return x

_drawn_inputs = setup_inputs


def setup_inputs(seed=0):
    import zlib

    import numpy as np

    out = dict(_drawn_inputs(seed))
    spreads = {}
    factors = {}
    for name, (base, spread) in spreads.items():
        noise = np.random.default_rng([zlib.crc32(name.encode()), seed]).standard_normal(out[name].shape)
        drawn = base * np.exp(spread * noise) if base else spread * noise
        out[name] = jnp.asarray(drawn.astype(out[name].dtype))
    for name, factor in factors.items():
        out[name] = (out[name] * factor).astype(out[name].dtype)
    return out
```

```python
import concourse.bass as bass
from concourse import mybir
from contextlib import ExitStack

FP32 = mybir.dt.float32
I32 = mybir.dt.int32
ALU = mybir.AluOpType
ACT = mybir.ActivationFunctionType
AX = mybir.AxisListType

EPS = 1e-5
P = 128
CH = 4
GE = CH * P
WIN = 24
SLOTS = 8
HALF = SLOTS // 2
BANK = 512
PAD_TYPE = 65536


def build(nc, x, src, dst, etype, W, out):
    N, D = x.shape
    E = src.shape[0]
    R = W.shape[0]
    KEYS = WIN * R
    GROUPS = -(-E // GE)
    ROUNDS = GROUPS // SLOTS
    REST = GROUPS - ROUNDS * SLOTS
    BLOCKS = -(-GROUPS // P)
    FULL = E // GE - (BLOCKS - 1) * P
    TAIL = E - (E // GE) * GE
    XT = N // ROUNDS
    assert XT * ROUNDS == N and XT <= P and TAIL > 0 and 0 < REST < SLOTS
    NODE_WINS = -(-N // BANK)
    ACC = NODE_WINS * BANK
    assert ACC >= N + WIN
    TILES = -(-N // P)
    PER = BANK // D
    BATCHES = -(-TILES // PER)

    ctx = ExitStack()
    with ctx:
        def sb(name, shape, dt=FP32):
            return ctx.enter_context(nc.sbuf_tensor(name, shape, dt))

        def ps(name):
            return ctx.enter_context(nc.psum_tensor(name, [P, BANK], FP32))

        def sem(name):
            return ctx.enter_context(nc.semaphore(name))

        src_raw = sb("src_raw", [P, BLOCKS, GE], I32)
        dst_raw = sb("dst_raw", [P, BLOCKS, GE], I32)
        typ_raw = sb("typ_raw", [P, BLOCKS, GE], I32)
        src_f = sb("src_f", [P, BLOCKS, GE])
        dst_f = sb("dst_f", [P, BLOCKS, GE])
        typ_f = sb("typ_f", [P, BLOCKS, GE])
        key_f = sb("key_f", [P, BLOCKS, GE])
        src_t = sb("src_t", [P, BLOCKS * P * CH], I32)
        key_t = sb("key_t", [P, BLOCKS * P * CH])
        typ_t = sb("typ_t", [P, BLOCKS * P * CH])
        dst_t = sb("dst_t", [P, BLOCKS * P * CH])
        bases = sb("bases", [1, GROUPS], I32)
        W_sb = sb("W_sb", [D, R, D])
        iota = sb("iota", [P, R * P])
        pid = sb("pid", [P, 1])
        ident = sb("ident", [P, P])
        ones = sb("ones", [P, 1])
        src_slot = sb("src_slot", [P, SLOTS, CH], I32)
        rows = sb("rows", [P, SLOTS, CH, D])
        onehot = sb("onehot", [P, HALF, CH, KEYS])
        z_sb = sb("z_sb", [D, 2, R, HALF, WIN])
        acc = sb("acc", [D, ACC])
        x_tile = sb("x_tile", [XT, D])
        stray = sb("stray", [P, BLOCKS * P * CH])
        lowest = sb("lowest", [P, 1])
        highest = sb("highest", [P, 1])
        far = sb("far", [P, 1])
        flag = sb("flag", [1, 1], I32)
        stats = sb("stats", [P, TILES, 6])
        mean_var = sb("mean_var", [P, BATCHES * PER, 2])
        eps = sb("eps", [P, 1])
        std = sb("std", [P, BATCHES * PER])
        rstd = sb("rstd", [P, BATCHES * PER])
        shift = sb("shift", [P, BATCHES * PER])
        y = sb("y", [P, 4, PER, D])
        st_z = sb("st_z", [D, R, P])
        st_msg = sb("st_msg", [P, CH, D])
        st_dst = sb("st_dst", [P, CH])
        st_key1h = key_f[:, 0:2, :].rearrange("p b e -> p (b e)")
        st_dst1h = src_f

        p_iota = ps("p_iota")
        p_turn = [ps("p_turn0"), ps("p_turn1")]
        p_z = [ps("p_z0"), ps("p_z1")]
        p_h = [ps("p_h0"), ps("p_h1")]
        p_x = ps("p_x")
        p_y = [p_turn[0], p_turn[1], p_z[0], p_z[1]]

        src_in = [sem(f"src_in{b}") for b in range(BLOCKS)]
        dst_typ_in = [sem(f"dst_typ_in{b}") for b in range(BLOCKS)]
        bases_in = sem("bases_in")
        w_in = sem("w_in")
        x_in = sem("x_in")
        pads_set = sem("pads_set")
        acc_zero = sem("acc_zero")
        iota_ready = sem("iota_ready")
        iota_in_psum = sem("iota_in_psum")
        ident_ready = sem("ident_ready")
        src_cast = sem("src_cast")
        lists_cast = sem("lists_cast")
        keyed = sem("keyed")
        prep = sem("prep")
        turned = sem("turned")
        turned_out = sem("turned_out")
        landed = [sem(f"landed{s}") for s in range(SLOTS)]
        idx_ready = [sem(f"idx_ready{s}") for s in range(SLOTS)]
        onehot_ready = sem("onehot_ready")
        z_ready = sem("z_ready")
        z_copied = sem("z_copied")
        h_ready = sem("h_ready")
        added = sem("added")
        x_turned = sem("x_turned")
        x_added = sem("x_added")
        far_counted = sem("far_counted")
        far_summed = sem("far_summed")
        flag_ready = sem("flag_ready")
        st_keyed = sem("st_keyed")
        st_idx = sem("st_idx")
        st_landed = sem("st_landed")
        st_onehot = sem("st_onehot")
        st_z_ready = sem("st_z_ready")
        st_z_copied = sem("st_z_copied")
        st_m_ready = sem("st_m_ready")
        st_m_copied = sem("st_m_copied")
        st_dstep = sem("st_dstep")
        st_win = sem("st_win")
        st_sum = sem("st_sum")
        st_added = sem("st_added")
        y_ready = sem("y_ready")
        aggregated = sem("aggregated")
        norm_known = sem("norm_known")
        std_known = sem("std_known")
        rstd_known = sem("rstd_known")
        stats_taken = sem("stats_taken")
        normed = sem("normed")
        stored = [sem(f"stored{i}") for i in range(4)]

        def n_stores(i, upto):
            n = 0
            for b in range(i, upto, 4):
                t0, t1 = b * PER, min(TILES, (b + 1) * PER)
                whole = min(t1, N // P)
                n += (whole > t0) + (whole < t1)
            return n

        def lists(name):
            return {"src": (src, src_raw), "dst": (dst, dst_raw), "typ": (etype, typ_raw)}[name]

        block = ctx.enter_context(nc.Block())

        @block.sync
        def _(sp):
            def load(name, b, done):
                dram, raw = lists(name)
                n = P if b < BLOCKS - 1 else FULL
                e0 = b * P * GE
                sp.dma_start(raw[0:n, b, :], dram[e0:e0 + n * GE].rearrange("(g e) -> g e", e=GE)).then_inc(done, 16)
                if b == BLOCKS - 1:
                    sp.dma_start(raw[n:n + 1, b, 0:TAIL],
                                 dram[e0 + n * GE:E].rearrange("(g e) -> g e", g=1)).then_inc(done, 16)

            load("src", 0, src_in[0])
            load("dst", 0, dst_typ_in[0])
            load("typ", 0, dst_typ_in[0])
            sp.dma_start(bases[0:1, 0:GROUPS - 1],
                         dst[0:(GROUPS - 1) * GE].rearrange("(o g e) -> o g e", o=1, e=GE)[:, :, 0],
                         allow_slow_non_contiguous=True).then_inc(bases_in, 16)
            sp.dma_start(bases[0:1, GROUPS - 1:GROUPS],
                         dst[(GROUPS - 1) * GE:(GROUPS - 1) * GE + 1].rearrange("(o g) -> o g", o=1)).then_inc(bases_in, 16)
            sp.dma_start(W_sb[:, :, :], W.rearrange("r i o -> i r o")).then_inc(w_in, 16)
            sp.dma_start(x_tile[:, :], x[0:XT, :]).then_inc(x_in, 16)
            sp.wait_ge(pads_set, 3)
            for b in range(1, BLOCKS):
                load("src", b, src_in[b])
                load("dst", b, dst_typ_in[b])
                load("typ", b, dst_typ_in[b])
            with sp.Fori(1, ROUNDS) as k:
                sp.wait_ge(x_turned, k)
                sp.dma_start(x_tile[:, :], x[bass.ds(k * XT, XT), :]).then_inc(x_in, 16)
            for b in range(BATCHES):
                t0, t1 = b * PER, min(TILES, (b + 1) * PER)
                whole = min(t1, N // P)
                sp.wait_ge(normed, t1)
                n_dma = 0
                if whole > t0:
                    sp.dma_start(out[t0 * P:whole * P, :].rearrange("(t p) d -> p t d", p=P),
                                 y[:, b % 4, 0:whole - t0, :]).then_inc(stored[b % 4], 16)
                if whole < t1:
                    sp.dma_start(out[whole * P:N, :], y[0:N - whole * P, b % 4, whole - t0, :]).then_inc(stored[b % 4], 16)
            for i in range(4):
                sp.wait_ge(stored[i], 16 * n_stores(i, BATCHES))

        @block.gpsimd
        def _(pool):
            pool.iota(iota[:, :], [[1, R * P]], base=0, channel_multiplier=0,
                      allow_small_or_imprecise_dtypes=True).then_inc(iota_ready, 1)
            pool.iota(pid[:, :], [[1, 1]], base=0, channel_multiplier=1,
                      allow_small_or_imprecise_dtypes=True).then_inc(iota_ready, 1)

            def gather(slot, idx, done):
                for j in range(CH):
                    pool.indirect_dma_start(rows[:, slot, j, :], None, x[:, :],
                                            bass.IndirectOffsetOnAxis(ap=idx[:, j:j + 1], axis=0)).then_inc(done, 16)

            pool.wait_ge(turned_out, 1)
            for s in range(SLOTS):
                gather(s, src_t[:, s * CH:(s + 1) * CH], landed[s])
            with pool.Fori(1, ROUNDS) as k:
                for s in range(SLOTS):
                    pool.wait_ge(turned_out, 1)
                    pool.wait_ge(idx_ready[s], k)
                    gather(s, src_slot[:, s, :], landed[s])
            for s in range(REST):
                pool.wait_ge(idx_ready[s], ROUNDS)
                gather(s, src_slot[:, s, :], landed[s])

            pool.wait_ge(flag_ready, 1)
            with pool.If(pool.value_load(flag[0:1, 0:1]) > 0):
                with pool.Fori(1, GROUPS + 1) as g1:
                    pool.wait_ge(turned_out, 1)
                    pool.wait_ge(st_idx, g1)
                    gather(0, src_slot[:, 0, :], st_landed)

        @block.scalar
        def _(act):
            for b in range(BLOCKS):
                act.wait_ge(src_in[b], 16 if b < BLOCKS - 1 else 32)
                nc.scalar.copy(src_f[:, b, :], src_raw[:, b, :]).then_inc(src_cast, 1)
                for q, table in enumerate((src_t, key_t, typ_t, dst_t)):
                    n = 4 * b + q
                    act.wait_ge(turned, n + 1)
                    nc.scalar.copy(table[:, b * GE:(b + 1) * GE].rearrange("p (g j) -> p g j", j=CH),
                                   p_turn[n % 2][:, :].rearrange("p (j g) -> p g j", j=CH)).then_inc(turned_out, 1)
                    if n == 0:
                        act.wait_ge(iota_ready, 2)
                        nc.scalar.copy(p_iota[:, 0:KEYS], iota[:, 0:KEYS]).then_inc(iota_in_psum, 1)

            def group(k, s, more):
                g = k * SLOTS + s
                half = s // HALF
                act.wait_ge(z_ready, g + 1)
                if s % HALF == 0 and not (isinstance(k, int) and k == 0):
                    act.wait_ge(h_ready, 2 * k + half - 1)
                nc.scalar.copy(z_sb[:, half, :, s % HALF, :],
                               p_z[s % 2][:, 0:KEYS].rearrange("p (d r) -> p r d", r=R)).then_inc(z_copied, 1)
                if more:
                    nc.scalar.copy(src_slot[:, s, :], src_t[:, bass.ds((g + SLOTS) * CH, CH)]).then_inc(idx_ready[s], 1)

            for s in range(SLOTS):
                group(0, s, True)
            with act.Fori(1, ROUNDS - 1) as k:
                for s in range(SLOTS):
                    group(k, s, True)
            for s in range(SLOTS):
                group(ROUNDS - 1, s, s < REST)
            for s in range(REST):
                group(ROUNDS, s, False)

            act.wait_ge(far_summed, 1)
            nc.scalar.copy(flag[0:1, 0:1], p_x[0:1, BANK - 1:BANK]).then_inc(flag_ready, 1)
            act.wait_ge(flag_ready, 1)
            with act.If(act.value_load(flag[0:1, 0:1]) > 0):
                def stray_group(g):
                    first = isinstance(g, int)
                    if not first:
                        act.wait_ge(st_z_ready, g * CH)
                    nc.scalar.copy(src_slot[:, 0, :], src_t[:, bass.ds(g * CH, CH)]).then_inc(st_idx, 1)
                    for j in range(CH):
                        act.wait_ge(st_z_ready, g * CH + (j + 1))
                        for h in range(2):
                            last = nc.scalar.copy(st_z[:, 4 * h:4 * h + 4, :],
                                                  p_turn[h][:, :].rearrange("p (r e) -> p r e", e=P))
                        last.then_inc(st_z_copied, 1)
                        act.wait_ge(st_m_ready, g * CH + (j + 1))
                        nc.scalar.copy(st_msg[:, j, :], p_z[0][:, 0:D]).then_inc(st_m_copied, 1)

                stray_group(0)
                with act.Fori(1, GROUPS) as g:
                    stray_group(g)

            def deviations(b):
                t0, t1 = b * PER, min(TILES, (b + 1) * PER)
                n = min(P, N - t0 * P)
                act.wait_ge(aggregated, t1)
                nc.scalar.activation(std[0:n, t0:t1], mean_var[0:n, t0:t1, 1], ACT.Sqrt,
                                     bias=eps[0:n, 0:1], scale=1.0).then_inc(std_known, 1)

            def normalise(b):
                act.wait_ge(norm_known, b + 1)
                if b >= 4:
                    act.wait_ge(stored[b % 4], 16 * n_stores(b % 4, b))
                for i in range(min(PER, TILES - b * PER)):
                    t = b * PER + i
                    n = min(P, N - t * P)
                    nc.scalar.activation(y[0:n, b % 4, i, :], p_y[b % 4][0:n, i * D:(i + 1) * D], ACT.Identity,
                                         bias=shift[0:n, t:t + 1], scale=rstd[0:n, t:t + 1]).then_inc(normed, 1)

            for b in range(BATCHES):
                deviations(b)
                if b >= 1:
                    normalise(b - 1)
            normalise(BATCHES - 1)

        @block.vector
        def _(dve):
            last = BLOCKS - 1
            nc.vector.memset(src_raw[:, last, :], 0).then_inc(pads_set, 1)
            nc.vector.memset(dst_raw[:, last, :], 0).then_inc(pads_set, 1)
            nc.vector.memset(typ_raw[:, last, :], PAD_TYPE).then_inc(pads_set, 1)
            nc.vector.memset(ones[:, :], 1.0).then_inc(acc_zero, 1)
            nc.vector.memset(eps[:, :], EPS).then_inc(acc_zero, 1)
            dve.wait_ge(iota_ready, 2)
            nc.vector.tensor_scalar(ident[:, :], iota[:, 0:P], pid[:, 0:1], None, ALU.is_equal).then_inc(ident_ready, 1)
            for b in range(BLOCKS):
                dve.wait_ge(dst_typ_in[b], 32 if b < last else 64)
                nc.vector.tensor_copy(dst_f[:, b, :], dst_raw[:, b, :]).then_inc(lists_cast, 1)
                nc.vector.tensor_copy(typ_f[:, b, :], typ_raw[:, b, :]).then_inc(lists_cast, 1)
                dve.wait_ge(lists_cast, 2 * b + 2)
                nc.vector.tensor_scalar(key_f[:, b, :], dst_f[:, b, :], dst_f[:, b, 0:1], float(R),
                                        ALU.subtract, ALU.mult).then_inc(prep, 1)
                dve.wait_ge(prep, b + 1)
                nc.vector.tensor_tensor(key_f[:, b, :], key_f[:, b, :], typ_f[:, b, :], ALU.add).then_inc(keyed, 1)
                if b == 0:
                    nc.vector.memset(acc[:, :], 0.0).then_inc(acc_zero, 1)
            dve.wait_ge(acc_zero, 3)
            dve.wait_ge(iota_in_psum, 1)

            def build_onehot(g, s):
                kt = key_t[:, bass.ds(g * CH, CH)]
                nc.vector.tensor_tensor(onehot[:, s % HALF, :, :],
                                        p_iota[:, 0:KEYS].unsqueeze(1).to_broadcast([P, CH, KEYS]),
                                        kt.unsqueeze(2).to_broadcast([P, CH, KEYS]), ALU.is_equal).then_inc(onehot_ready, 1)

            def add_windows(h, half, n, first=False):
                for i in range(n):
                    g = h * HALF + i
                    base = dve.value_load(bases[0:1, bass.ds(g, 1)], min_val=0, max_val=N - 1)
                    if not (first and i == 0):
                        dve.wait_ge(added, g)
                    dve.wait_ge(h_ready, h + 1)
                    window = acc[:, bass.ds(base, WIN)]
                    nc.vector.tensor_tensor(window, window, p_h[half][:, i * WIN:(i + 1) * WIN], ALU.add).then_inc(added, 1)

            def half_round(k, half, n=HALF):
                for s in range(half * HALF, half * HALF + n):
                    g = k * SLOTS + s
                    if not (isinstance(k, int) and g < HALF):
                        dve.wait_ge(z_ready, g - (HALF - 1))
                    build_onehot(g, s)
                if not (isinstance(k, int) and k == 0):
                    add_windows(2 * k + half - 2, half, HALF, isinstance(k, int) and k == 1 and half == 0)

            def add_residual(k):
                dve.wait_ge(x_turned, k + 1)
                if not (isinstance(k, int) and k == 0):
                    dve.wait_ge(added, k * SLOTS)
                nodes = acc[:, bass.ds(k * XT, XT)]
                nc.vector.scalar_tensor_tensor(nodes, p_x[:, 0:XT], 2.0, nodes, ALU.mult, ALU.add).then_inc(x_added, 1)
                dve.wait_ge(x_added, k + 1)

            dve.wait_ge(turned_out, 2)
            dve.wait_ge(bases_in, 32)
            half_round(0, 0)
            half_round(0, 1)
            add_residual(0)
            dve.wait_ge(turned_out, 4 * BLOCKS)
            nc.vector.scalar_tensor_tensor(stray[:, :], key_t[:, :], float(PAD_TYPE - R * N), key_t[:, :],
                                           ALU.is_lt, ALU.mult).then_inc(prep, 1)
            nc.vector.tensor_reduce(lowest[:, :], key_t[:, :], AX.X, ALU.min).then_inc(prep, 1)
            dve.wait_ge(prep, BLOCKS + 2)
            nc.vector.tensor_reduce(highest[:, :], stray[:, :], AX.X, ALU.max).then_inc(prep, 1)
            nc.vector.tensor_scalar(far[:, :], lowest[:, :], 0.0, None, ALU.is_lt).then_inc(prep, 1)
            dve.wait_ge(prep, BLOCKS + 4)
            nc.vector.scalar_tensor_tensor(far[:, :], highest[:, :], float(KEYS), far[:, :],
                                           ALU.is_ge, ALU.add).then_inc(far_counted, 1)
            half_round(1, 0)
            half_round(1, 1)
            add_residual(1)
            with dve.Fori(2, ROUNDS) as k:
                half_round(k, 0)
                half_round(k, 1)
                add_residual(k)
            half_round(ROUNDS, 0, REST)
            add_windows(2 * ROUNDS - 1, 1, HALF)
            add_windows(2 * ROUNDS, 0, REST)

            dve.wait_ge(added, GROUPS)
            dve.wait_ge(flag_ready, 1)
            with dve.If(dve.value_load(flag[0:1, 0:1]) > 0):
                nc.vector.tensor_scalar(stray[:, :], key_t[:, :], 0.0, None, ALU.is_lt).then_inc(st_keyed, 1)
                nc.vector.tensor_scalar(typ_t[:, :], typ_t[:, :], float(P), pid[:, 0:1], ALU.mult, ALU.add).then_inc(st_keyed, 1)
                dve.wait_ge(st_keyed, 2)
                nc.vector.scalar_tensor_tensor(stray[:, :], key_t[:, :], float(KEYS), stray[:, :],
                                               ALU.is_ge, ALU.add).then_inc(st_keyed, 1)
                nc.vector.tensor_scalar(typ_t[:, :], typ_t[:, :], 1.0, None, ALU.add).then_inc(st_keyed, 1)
                dve.wait_ge(st_keyed, 4)
                nc.vector.tensor_tensor(stray[:, :], stray[:, :], typ_t[:, :], ALU.mult).then_inc(st_keyed, 1)
                dve.wait_ge(st_keyed, 5)
                nc.vector.tensor_scalar(stray[:, :], stray[:, :], -1.0, None, ALU.add).then_inc(st_keyed, 1)
                dve.wait_ge(st_keyed, 6)

                def stray_group(g):
                    first = isinstance(g, int)
                    for j in range(CH):
                        if not (first and j == 0):
                            dve.wait_ge(st_z_ready, g * CH + j)
                        nc.vector.tensor_tensor(st_key1h, iota[:, :],
                                                stray[:, bass.ds(g * CH + j, 1)].to_broadcast([P, R * P]),
                                                ALU.is_equal).then_inc(st_onehot, 1)
                    if not first:
                        dve.wait_ge(st_added, g * NODE_WINS)
                    if not first:
                        dve.wait_ge(st_dstep, g * NODE_WINS)
                    nc.vector.tensor_copy(st_dst[:, :], dst_t[:, bass.ds(g * CH, CH)]).then_inc(st_keyed, 1)
                    with dve.Fori(0, NODE_WINS) as w:
                        n = g * NODE_WINS + w
                        dve.wait_ge(st_keyed, g + 7)
                        nc.vector.tensor_tensor(st_dst1h[:, :, :],
                                                iota[:, 0:BANK].unsqueeze(1).to_broadcast([P, CH, BANK]),
                                                st_dst[:, :].unsqueeze(2).to_broadcast([P, CH, BANK]),
                                                ALU.is_equal).then_inc(st_win, 1)
                        dve.wait_ge(st_win, n + 1)
                        nc.vector.tensor_scalar(st_dst[:, :], st_dst[:, :], float(-BANK), None,
                                                ALU.add).then_inc(st_dstep, 1)
                        dve.wait_ge(st_dstep, n + 1)
                        dve.wait_ge(st_sum, n + 1)
                        nodes = acc[:, bass.ds(w * BANK, BANK)]
                        nc.vector.tensor_tensor(nodes, nodes, p_z[1][:, :], ALU.add).then_inc(st_added, 1)

                stray_group(0)
                with dve.Fori(1, GROUPS) as g:
                    stray_group(g)
                dve.wait_ge(st_added, GROUPS * NODE_WINS)

            def take_stats(b):
                tiles = range(b * PER, min(TILES, (b + 1) * PER))
                dve.wait_ge(y_ready, b + 1)
                for i, t in enumerate(tiles):
                    n = min(P, N - t * P)
                    nc.vector.bn_stats(stats[0:n, t, :], p_y[b % 4][0:n, i * D:(i + 1) * D]).then_inc(stats_taken, 1)
                for i, t in enumerate(tiles):
                    n = min(P, N - t * P)
                    dve.wait_ge(stats_taken, t + 1)
                    nc.vector.bn_aggr(mean_var[0:n, t, :], stats[0:n, t, :]).then_inc(aggregated, 1)

            def finish(b):
                t0, t1 = b * PER, min(TILES, (b + 1) * PER)
                n = min(P, N - t0 * P)
                dve.wait_ge(std_known, b + 1)
                nc.vector.reciprocal(rstd[0:n, t0:t1], std[0:n, t0:t1]).then_inc(rstd_known, 1)
                dve.wait_ge(rstd_known, b + 1)
                nc.vector.scalar_tensor_tensor(shift[0:n, t0:t1], mean_var[0:n, t0:t1, 0], -1.0, rstd[0:n, t0:t1],
                                               ALU.mult, ALU.mult).then_inc(norm_known, 1)

            for b in range(BATCHES):
                take_stats(b)
                if b >= 1:
                    finish(b - 1)
            finish(BATCHES - 1)

        @block.tensor
        def _(pe):
            pe.wait_ge(ident_ready, 1)
            for b in range(BLOCKS):
                for q, listed in enumerate((src_f, key_f, typ_f, dst_f)):
                    n = 4 * b + q
                    if q == 0:
                        pe.wait_ge(src_cast, b + 1)
                    if q == 1:
                        pe.wait_ge(keyed, b + 1)
                    if n >= 2:
                        pe.wait_ge(turned_out, n - 1)
                    for j in range(CH):
                        last = nc.tensor.transpose(p_turn[n % 2][:, j * P:(j + 1) * P], listed[:, b, j * P:(j + 1) * P],
                                                   ident[:, :])
                    last.then_inc(turned, 1)

            def sums(k, s):
                g = k * SLOTS + s
                pe.wait_ge(landed[s], (k + 1) * (16 * CH))
                pe.wait_ge(onehot_ready, g + 1)
                if not (isinstance(k, int) and g < 2):
                    pe.wait_ge(z_copied, g - 1)
                for j in range(CH):
                    last = nc.tensor.matmul(p_z[s % 2][:, 0:KEYS], rows[:, s, j, :], onehot[:, s % HALF, j, :],
                                            start=(j == 0), stop=(j == CH - 1))
                last.then_inc(z_ready, 1)

            def products(h, half, n=HALF):
                pe.wait_ge(z_copied, h * HALF + n)
                if not (isinstance(h, int) and h < 2):
                    pe.wait_ge(added, (h - 1) * HALF)
                for r in range(R):
                    last = nc.tensor.matmul(p_h[half][:, 0:n * WIN], W_sb[:, r, :],
                                            z_sb[:, half, r, 0:n, :].rearrange("p i d -> p (i d)"),
                                            start=(r == 0), stop=(r == R - 1))
                last.then_inc(h_ready, 1)

            def turn_x(k):
                pe.wait_ge(x_in, (k + 1) * 16)
                if not isinstance(k, int):
                    pe.wait_ge(x_added, k)
                nc.tensor.transpose(p_x[:, 0:XT], x_tile[:, :], ident[0:XT, 0:XT]).then_inc(x_turned, 1)

            def round_(k):
                for s in range(HALF):
                    sums(k, s)
                if not (isinstance(k, int) and k == 0):
                    products(2 * k - 1, 1)
                turn_x(k)
                for s in range(HALF, SLOTS):
                    sums(k, s)
                products(2 * k, 0)

            pe.wait_ge(w_in, 16)
            round_(0)
            with pe.Fori(1, ROUNDS) as k:
                round_(k)
            for s in range(REST):
                sums(ROUNDS, s)
            products(2 * ROUNDS - 1, 1)
            products(2 * ROUNDS, 0, REST)

            pe.wait_ge(far_counted, 1)
            pe.wait_ge(x_added, ROUNDS)
            nc.tensor.matmul(p_x[0:1, BANK - 1:BANK], far[:, :], ones[:, :], start=True, stop=True).then_inc(far_summed, 1)

            pe.wait_ge(flag_ready, 1)
            with pe.If(pe.value_load(flag[0:1, 0:1]) > 0):
                def stray_group(g):
                    pe.wait_ge(st_landed, (g + 1) * (16 * CH))
                    for j in range(CH):
                        pe.wait_ge(st_onehot, g * CH + (j + 1))
                        for h in range(2):
                            last = nc.tensor.matmul(p_turn[h][:, :], rows[:, 0, j, :], st_key1h[:, h * BANK:(h + 1) * BANK],
                                                    start=True, stop=True)
                        last.then_inc(st_z_ready, 1)
                        pe.wait_ge(st_z_copied, g * CH + (j + 1))
                        if j >= 1:
                            pe.wait_ge(st_m_copied, g * CH + j)
                        for r in range(R):
                            last = nc.tensor.matmul(p_z[0][:, 0:D], st_z[:, r, :], W_sb[:, r, :],
                                                    start=(r == 0), stop=(r == R - 1))
                        last.then_inc(st_m_ready, 1)
                    with pe.Fori(0, NODE_WINS) as w:
                        pe.wait_ge(st_m_copied, (g + 1) * CH)
                        pe.wait_ge(st_win, g * NODE_WINS + w + 1)
                        for j in range(CH):
                            last = nc.tensor.matmul(p_z[1][:, :], st_msg[:, j, :], st_dst1h[:, j, :],
                                                    start=(j == 0), stop=(j == CH - 1))
                        last.then_inc(st_sum, 1)

                stray_group(0)
                with pe.Fori(1, GROUPS) as g:
                    stray_group(g)
                pe.wait_ge(st_added, GROUPS * NODE_WINS)

            pe.wait_ge(added, GROUPS)
            for b in range(BATCHES):
                if b >= 4:
                    pe.wait_ge(normed, (b - 3) * PER)
                for i in range(min(PER, TILES - b * PER)):
                    t = b * PER + i
                    n = min(P, N - t * P)
                    last = nc.tensor.transpose(p_y[b % 4][0:n, i * D:(i + 1) * D], acc[:, t * P:t * P + n], ident[:, :])
                last.then_inc(y_ready, 1)


def kernel(x, src, dst, edge_type_8, L0_gnn_W):
    import numpy as np
    import concourse.bacc as bacc
    from concourse.bass_utils import run_bass_kernel_spmd

    nc = bacc.Bacc("TRN2", target_bir_lowering=False, num_devices=1)
    arrays, args = {}, []
    for name, a in (("x", x), ("src", src), ("dst", dst), ("edge_type", edge_type_8), ("W", L0_gnn_W)):
        a = np.ascontiguousarray(a)
        arrays[f"in_{name}"] = a
        args.append(nc.dram_tensor(f"in_{name}", a.shape, mybir.dt.from_np(a.dtype), kind="ExternalInput").ap())
    args.append(nc.dram_tensor("out_0", arrays["in_x"].shape, FP32, kind="ExternalOutput").ap())
    build(nc, *args)
    return run_bass_kernel_spmd(nc, [arrays], core_ids=[0]).results[0]["out_0"]
```

```python
import concourse.bass as bass
from concourse import mybir
from contextlib import ExitStack

FP32 = mybir.dt.float32
BF16 = mybir.dt.bfloat16
I32 = mybir.dt.int32
I16 = mybir.dt.int16
ALU = mybir.AluOpType
ACT = mybir.ActivationFunctionType
AX = mybir.AxisListType

EPS = 1e-5
P = 128
CH = 4
GE = CH * P
WIN = 24
SLOTS = 8
TURN = 16
QUART = 4
PARTS = 3
BANK = 512
PAD_DST = 32767


def build(nc, x, src, dst, etype, W, out):
    N, D = x.shape
    E = src.shape[0]
    R = W.shape[0]
    KEYS = WIN * R
    GROUPS = -(-E // GE)
    BLOCKS = -(-GROUPS // P)
    FULL = E // GE - (BLOCKS - 1) * P
    TAIL = E - (E // GE) * GE
    TURNS = GROUPS // (TURN + 1)
    DENSE = TURNS
    GATHERED = GROUPS - DENSE
    REST = GATHERED - TURNS * TURN
    ROUNDS = GATHERED // SLOTS
    assert REST == 3 * QUART and GATHERED - ROUNDS * SLOTS == QUART and TAIL > 0
    NODE_WINS = -(-N // BANK)
    ACC = NODE_WINS * BANK
    TILES = -(-N // P)
    LAST = N - (TILES - 1) * P
    PER = BANK // D
    BATCHES = -(-TILES // PER)
    SPLITS = 7
    ST = TILES // SPLITS
    assert ACC >= N + WIN and ST * SPLITS == TILES
    KEY_END = R * N
    assert (PAD_DST - N) * R > KEY_END and PAD_DST >= ACC
    CUTS = [0, 13, 25, 37, TILES]
    PIECES = len(CUTS) - 1
    WIDE = max(b - a for a, b in zip(CUTS, CUTS[1:]))
    SLOT_PIECES = [[n] for n in range(14)] + [[14, 15], []]

    ctx = ExitStack()
    with ctx:
        def sb(name, shape, dt=FP32):
            return ctx.enter_context(nc.sbuf_tensor(name, shape, dt))

        def ps(name):
            return ctx.enter_context(nc.psum_tensor(name, [P, BANK], FP32))

        def sem(name):
            return ctx.enter_context(nc.semaphore(name))

        acc = sb("acc", [D, ACC])
        raw = acc[:, 0:3 * BLOCKS * GE].bitcast(I32).rearrange("p (l b e) -> p l b e", l=3, b=BLOCKS)
        src_raw, dst_raw, typ_raw = (raw[:, i, :, :] for i in range(3))
        stage = sb("stage", [P, 4 * BLOCKS * GE])
        lists_f = stage[:, :].rearrange("p (l b e) -> p l b e", l=4, b=BLOCKS)
        src_f, key_f, typ_f, dst_f = (lists_f[:, i, :, :] for i in range(4))
        x_f = stage[:, 0:TILES * D].rearrange("p (t d) -> p t d", d=D)
        COLS = BLOCKS * P * CH
        stray = stage[:, 0:COLS]
        outside = stage[:, COLS:2 * COLS]
        st_dst1h = stage[:, COLS:COLS + CH * BANK].rearrange("p (j n) -> p j n", j=CH)
        st_key1h = stage[:, 2 * COLS:2 * COLS + R * P]
        st_z = stage[:, 2 * COLS + R * P:2 * COLS + 2 * R * P].rearrange("p (r e) -> p r e", r=R)
        st_msg = stage[:, 2 * COLS + 2 * R * P:2 * COLS + 2 * R * P + CH * D].rearrange("p (j d) -> p j d", j=CH)
        y = stage[:, 0:4 * PER * D].rearrange("p (b i d) -> p b i d", b=4, i=PER)
        src_t = sb("src_t", [P, COLS], I16)
        key_t = sb("key_t", [P, COLS])
        typ_t = sb("typ_t", [P, COLS], I16)
        dst_t = sb("dst_t", [P, COLS], I16)
        bases = sb("bases", [1, GROUPS], I32)
        W_sb = sb("W_sb", [D, R, D])
        x_parts = sb("x_parts", [P, TILES, PARTS, D], BF16)
        iota = sb("iota", [P, R * P])
        nodes_of = sb("nodes_of", [P, TILES])
        pid = sb("pid", [P, 1])
        pid1 = sb("pid1", [P, 1])
        ident = sb("ident", [P, P])
        ident2 = sb("ident2", [P, P], BF16)
        ones = sb("ones", [P, 1])
        src_slot = sb("src_slot", [P, SLOTS + 1, CH], I32)
        rows = sb("rows", [P, SLOTS, CH, D])
        rows_d = sb("rows_d", [P, CH, D])
        src_b = sb("src_b", [P, 2, P], I32)
        node1h = sb("node1h", [P, 2, WIDE, P], BF16)
        onehot = sb("onehot", [P, QUART + 1, CH, KEYS])
        z_sb = sb("z_sb", [D, 2, R, QUART + 1, WIN])
        far_key = sb("far_key", [P, GE])
        lowest = sb("lowest", [P, BLOCKS])
        highest = sb("highest", [P, BLOCKS])
        low_high = sb("low_high", [P, 2])
        far = sb("far", [P, 1])
        flag = sb("flag", [1, 1], I32)
        stats = sb("stats", [P, TILES, 6])
        mean_var = sb("mean_var", [P, BATCHES * PER, 2])
        eps = sb("eps", [P, 1])
        std = sb("std", [P, BATCHES * PER])
        rstd = sb("rstd", [P, BATCHES * PER])
        shift = sb("shift", [P, BATCHES * PER])
        st_dst = sb("st_dst", [P, CH])

        p_const = ps("p_const")
        key_iota = p_const[:, 0:KEYS]
        tile_nodes = p_const[:, BANK // 2:BANK // 2 + TILES]
        p_flag = p_const[0:1, BANK - 1:BANK]
        p_turn = [ps("p_turn0"), ps("p_turn1")]
        p_z = [ps("p_z0"), ps("p_z1")]
        p_zd = ps("p_zd")[:, 0:KEYS]
        p_h = [ps("p_h0"), ps("p_h1")]
        p_y = [p_turn[0], p_turn[1], p_z[0], p_z[1]]

        src_in = [sem(f"src_in{b}") for b in range(BLOCKS)]
        dst_typ_in = [sem(f"dst_typ_in{b}") for b in range(BLOCKS)]
        bases_in = sem("bases_in")
        w_in = sem("w_in")
        x_in = sem("x_in")
        src_b_in = [sem("src_b_in0"), sem("src_b_in1")]
        pads_set = sem("pads_set")
        acc_zero = sem("acc_zero")
        iota_ready = sem("iota_ready")
        const_in_psum = sem("const_in_psum")
        ident_ready = sem("ident_ready")
        src_cast = sem("src_cast")
        lists_cast = sem("lists_cast")
        keyed = sem("keyed")
        prep = sem("prep")
        turned = sem("turned")
        turned_out = sem("turned_out")
        far_parts = sem("far_parts")
        far_counted = sem("far_counted")
        far_summed = sem("far_summed")
        flag_ready = sem("flag_ready")
        x_pad = sem("x_pad")
        x_hi = sem("x_hi")
        x_less_hi = sem("x_less_hi")
        x_mid = sem("x_mid")
        x_split = sem("x_split")
        res_ready = sem("res_ready")
        res_added = sem("res_added")
        landed = [sem(f"landed{s}") for s in range(SLOTS)]
        landed_d = sem("landed_d")
        idx_ready = [sem(f"idx_ready{s}") for s in range(SLOTS)]
        onehot_ready = sem("onehot_ready")
        z_ready = sem("z_ready")
        z_copied = sem("z_copied")
        h_ready = sem("h_ready")
        added = sem("added")
        node1h_ready = sem("node1h_ready")
        node1h_used = sem("node1h_used")
        rows_built = sem("rows_built")
        st_keyed = sem("st_keyed")
        st_idx = sem("st_idx")
        st_landed = sem("st_landed")
        st_onehot = sem("st_onehot")
        st_z_ready = sem("st_z_ready")
        st_z_copied = sem("st_z_copied")
        st_m_ready = sem("st_m_ready")
        st_m_copied = sem("st_m_copied")
        st_dstep = sem("st_dstep")
        st_win = sem("st_win")
        st_sum = sem("st_sum")
        st_added = sem("st_added")
        y_ready = sem("y_ready")
        aggregated = sem("aggregated")
        norm_known = sem("norm_known")
        std_known = sem("std_known")
        rstd_known = sem("rstd_known")
        stats_taken = sem("stats_taken")
        normed = sem("normed")
        stored = [sem(f"stored{i}") for i in range(4)]

        def is0(k):
            return isinstance(k, int) and k == 0

        def pos(k, s):
            return s if is0(k) else k * (TURN + 1) + (s - 1 + (s >= QUART))

        def pos_d(k):
            return k * (TURN + 1) + (QUART - 1)

        def through(k, q):
            return k * (TURN + 1) + QUART * (q + 1)

        def two_back(k, q):
            return (k, q - 2) if q >= 2 else (k - 1, q + 2)

        def n_stores(i, upto):
            n = 0
            for b in range(i, upto, 4):
                t0, t1 = b * PER, min(TILES, (b + 1) * PER)
                whole = min(t1, N // P)
                n += (whole > t0) + (whole < t1)
            return n

        block = ctx.enter_context(nc.Block())

        @block.sync
        def _(sp):
            def load(dram, into, b, done):
                n = P if b < BLOCKS - 1 else FULL
                e0 = b * P * GE
                sp.dma_start(into[0:n, b, :], dram[e0:e0 + n * GE].rearrange("(g e) -> g e", e=GE)).then_inc(done, 16)
                if b == BLOCKS - 1:
                    sp.dma_start(into[n:n + 1, b, 0:TAIL],
                                 dram[e0 + n * GE:E].rearrange("(g e) -> g e", g=1)).then_inc(done, 16)

            load(src, src_raw, 0, src_in[0])
            load(dst, dst_raw, 0, dst_typ_in[0])
            load(etype, typ_raw, 0, dst_typ_in[0])
            sp.wait_ge(pads_set, 3)
            for b in range(1, BLOCKS):
                load(src, src_raw, b, src_in[b])
                load(dst, dst_raw, b, dst_typ_in[b])
                load(etype, typ_raw, b, dst_typ_in[b])
            sp.dma_start(bases[0:1, 0:GROUPS - 1],
                         dst[0:(GROUPS - 1) * GE].rearrange("(o g e) -> o g e", o=1, e=GE)[:, :, 0],
                         allow_slow_non_contiguous=True).then_inc(bases_in, 16)
            sp.dma_start(bases[0:1, GROUPS - 1:GROUPS],
                         dst[(GROUPS - 1) * GE:(GROUPS - 1) * GE + 1].rearrange("(o g) -> o g", o=1)).then_inc(bases_in, 16)
            sp.dma_start(W_sb[:, :, :], W.rearrange("r i o -> i r o")).then_inc(w_in, 16)
            sp.wait_ge(x_pad, 1)
            sp.dma_start(x_f[:, 0:TILES - 1, :],
                         x[0:(TILES - 1) * P, :].rearrange("(t p) d -> p t d", p=P)).then_inc(x_in, 16)
            sp.dma_start(x_f[0:LAST, TILES - 1, :], x[(TILES - 1) * P:N, :]).then_inc(x_in, 16)

            def spread_src(k):
                for j in range(CH):
                    if not (isinstance(k, int) and j < 2):
                        sp.wait_ge(node1h_ready, (k - 1) * (CH * PIECES) + (j - 1) * PIECES)
                    sp.dma_start(src_b[:, j % 2, :],
                                 src[bass.ds(k * GE + j * P, P)].rearrange("(o e) -> o e", o=1).to_broadcast([P, P])
                                 ).then_inc(src_b_in[j % 2], 16)

            spread_src(1)
            with sp.Fori(2, TURNS) as k:
                spread_src(k)
            for b in range(BATCHES):
                t0, t1 = b * PER, min(TILES, (b + 1) * PER)
                whole = min(t1, N // P)
                sp.wait_ge(normed, t1)
                if whole > t0:
                    sp.dma_start(out[t0 * P:whole * P, :].rearrange("(t p) d -> p t d", p=P),
                                 y[:, b % 4, 0:whole - t0, :]).then_inc(stored[b % 4], 16)
                if whole < t1:
                    sp.dma_start(out[whole * P:N, :], y[0:N - whole * P, b % 4, whole - t0, :]).then_inc(stored[b % 4], 16)
            for i in range(4):
                sp.wait_ge(stored[i], 16 * n_stores(i, BATCHES))

        @block.gpsimd
        def _(pool):
            pool.iota(iota[:, :], [[1, R * P]], base=0, channel_multiplier=0,
                      allow_small_or_imprecise_dtypes=True).then_inc(iota_ready, 1)
            pool.iota(pid[:, :], [[1, 1]], base=0, channel_multiplier=1,
                      allow_small_or_imprecise_dtypes=True).then_inc(iota_ready, 1)
            pool.iota(pid1[:, :], [[1, 1]], base=1, channel_multiplier=1,
                      allow_small_or_imprecise_dtypes=True).then_inc(iota_ready, 1)
            pool.iota(nodes_of[:, :], [[P, TILES]], base=0, channel_multiplier=1,
                      allow_small_or_imprecise_dtypes=True).then_inc(iota_ready, 1)

            def gather(into, slot, done):
                for j in range(CH):
                    pool.indirect_dma_start(into[:, j, :], None, x[:, :],
                                            bass.IndirectOffsetOnAxis(ap=src_slot[:, slot, j:j + 1], axis=0)).then_inc(done, 16)

            pool.wait_ge(turned_out, 1)
            for s in range(SLOTS):
                pool.wait_ge(idx_ready[s], 1)
                gather(rows[:, s, :, :], s, landed[s])
            gather(rows_d, SLOTS, landed_d)
            with pool.Fori(2, ROUNDS + 1) as k:
                for s in range(SLOTS):
                    pool.wait_ge(turned_out, 1)
                    pool.wait_ge(idx_ready[s], k)
                    gather(rows[:, s, :, :], s, landed[s])
            for s in range(QUART):
                pool.wait_ge(idx_ready[s], ROUNDS + 1)
                gather(rows[:, s, :, :], s, landed[s])

            pool.wait_ge(flag_ready, 1)
            with pool.If(pool.value_load(flag[0:1, 0:1]) > 0):
                with pool.Fori(1, GROUPS + 1) as g1:
                    pool.wait_ge(turned_out, 1)
                    pool.wait_ge(st_idx, g1)
                    gather(rows[:, 0, :, :], 0, st_landed)

        @block.scalar
        def _(act):
            for b in range(BLOCKS):
                act.wait_ge(src_in[b], 16 if b < BLOCKS - 1 else 32)
                nc.scalar.copy(src_f[:, b, :], src_raw[:, b, :]).then_inc(src_cast, 1)
                for q, table in enumerate((src_t, key_t, typ_t, dst_t)):
                    n = 4 * b + q
                    act.wait_ge(turned, n + 1)
                    nc.scalar.copy(table[:, b * GE:(b + 1) * GE].rearrange("p (g j) -> p g j", j=CH),
                                   p_turn[n % 2][:, :].rearrange("p (j g) -> p g j", j=CH)).then_inc(turned_out, 1)
                    if n == 0:
                        act.wait_ge(turned_out, 1)
                        nc.scalar.copy(src_slot[:, SLOTS, :], src_t[:, 0:CH])
                        for s in range(SLOTS):
                            nc.scalar.copy(src_slot[:, s, :], src_t[:, (DENSE + s) * CH:(DENSE + s + 1) * CH]
                                           ).then_inc(idx_ready[s], 1)
                        act.wait_ge(iota_ready, 4)
                        nc.scalar.copy(key_iota, iota[:, 0:KEYS]).then_inc(const_in_psum, 1)
                        nc.scalar.copy(tile_nodes, nodes_of[:, :]).then_inc(const_in_psum, 1)

            def quarter(k, q, refill=True, n=QUART):
                for i in range(n):
                    s = q * QUART + i
                    act.wait_ge(z_ready, pos(k, s) + 1)
                    if i == 0 and not (is0(k) and q < 2):
                        act.wait_ge(h_ready, 4 * k + (q - 1))
                    nc.scalar.copy(z_sb[:, q % 2, :, i, :],
                                   p_z[s % 2][:, 0:KEYS].rearrange("p (d r) -> p r d", r=R)).then_inc(z_copied, 1)
                    if refill:
                        g = k * TURN + (DENSE + s + SLOTS)
                        nc.scalar.copy(src_slot[:, s % SLOTS, :], src_t[:, bass.ds(g * CH, CH)]
                                       ).then_inc(idx_ready[s % SLOTS], 1)
                    if is0(k):
                        split(s)
                if q == 0 and not is0(k):
                    act.wait_ge(z_ready, pos_d(k) + 1)
                    nc.scalar.copy(z_sb[:, 0, :, QUART, :],
                                   p_zd.rearrange("p (d r) -> p r d", r=R)).then_inc(z_copied, 1)

            def split(s):
                i = s - 4
                if 0 <= i < SPLITS:
                    act.wait_ge(x_in, 32)
                    nc.scalar.copy(x_parts[:, i * ST:(i + 1) * ST, 0, :], x_f[:, i * ST:(i + 1) * ST, :]).then_inc(x_hi, 1)
                i = s - 5
                if 0 <= i < SPLITS:
                    act.wait_ge(x_less_hi, i + 1)
                    nc.scalar.copy(x_parts[:, i * ST:(i + 1) * ST, 1, :], x_f[:, i * ST:(i + 1) * ST, :]).then_inc(x_mid, 1)

            for q in range(4):
                quarter(0, q)
            with act.Fori(1, TURNS) as k:
                for q in range(4):
                    quarter(k, q)
            quarter(TURNS, 0)
            quarter(TURNS, 1, refill=False)
            quarter(TURNS, 2, refill=False)

            act.wait_ge(far_summed, 1)
            nc.scalar.copy(flag[0:1, 0:1], p_flag).then_inc(flag_ready, 1)
            act.wait_ge(flag_ready, 1)
            with act.If(act.value_load(flag[0:1, 0:1]) > 0):
                def stray_group(g):
                    if not isinstance(g, int):
                        act.wait_ge(st_z_ready, g * CH)
                    nc.scalar.copy(src_slot[:, 0, :], src_t[:, bass.ds(g * CH, CH)]).then_inc(st_idx, 1)
                    for j in range(CH):
                        act.wait_ge(st_z_ready, g * CH + (j + 1))
                        for h in range(2):
                            last = nc.scalar.copy(st_z[:, 4 * h:4 * h + 4, :],
                                                  p_turn[h][:, :].rearrange("p (r e) -> p r e", e=P))
                        last.then_inc(st_z_copied, 1)
                        act.wait_ge(st_m_ready, g * CH + (j + 1))
                        nc.scalar.copy(st_msg[:, j, :], p_z[0][:, 0:D]).then_inc(st_m_copied, 1)

                stray_group(0)
                with act.Fori(1, GROUPS) as g:
                    stray_group(g)

            def deviations(b):
                t0, t1 = b * PER, min(TILES, (b + 1) * PER)
                n = min(P, N - t0 * P)
                act.wait_ge(aggregated, t1)
                nc.scalar.activation(std[0:n, t0:t1], mean_var[0:n, t0:t1, 1], ACT.Sqrt,
                                     bias=eps[0:n, 0:1], scale=1.0).then_inc(std_known, 1)

            def normalise(b):
                act.wait_ge(norm_known, b + 1)
                if b >= 4:
                    act.wait_ge(stored[b % 4], 16 * n_stores(b % 4, b))
                for i in range(min(PER, TILES - b * PER)):
                    t = b * PER + i
                    n = min(P, N - t * P)
                    nc.scalar.activation(y[0:n, b % 4, i, :], p_y[b % 4][0:n, i * D:(i + 1) * D], ACT.Identity,
                                         bias=shift[0:n, t:t + 1], scale=rstd[0:n, t:t + 1]).then_inc(normed, 1)

            for b in range(BATCHES):
                deviations(b)
                if b >= 1:
                    normalise(b - 1)
            normalise(BATCHES - 1)

        @block.vector
        def _(dve):
            last = BLOCKS - 1
            nc.vector.memset(src_raw[:, last, :], 0).then_inc(pads_set, 1)
            nc.vector.memset(dst_raw[:, last, :], PAD_DST).then_inc(pads_set, 1)
            nc.vector.memset(typ_raw[:, last, :], 0).then_inc(pads_set, 1)
            nc.vector.memset(ones[:, :], 1.0).then_inc(acc_zero, 1)
            nc.vector.memset(eps[:, :], EPS).then_inc(acc_zero, 1)
            dve.wait_ge(iota_ready, 4)
            nc.vector.tensor_scalar(ident[:, :], iota[:, 0:P], pid[:, 0:1], None, ALU.is_equal).then_inc(ident_ready, 1)
            nc.vector.tensor_scalar(ident2[:, :], iota[:, 0:P], pid[:, 0:1], 2.0, ALU.is_equal, ALU.mult).then_inc(ident_ready, 1)
            for b in range(BLOCKS):
                dve.wait_ge(dst_typ_in[b], 32 if b < last else 64)
                nc.vector.tensor_copy(dst_f[:, b, :], dst_raw[:, b, :]).then_inc(lists_cast, 1)
                nc.vector.tensor_copy(typ_f[:, b, :], typ_raw[:, b, :]).then_inc(lists_cast, 1)
                dve.wait_ge(lists_cast, 2 * b + 2)
                nc.vector.tensor_scalar(key_f[:, b, :], dst_f[:, b, :], dst_f[:, b, 0:1], float(R),
                                        ALU.subtract, ALU.mult).then_inc(prep, 1)
                dve.wait_ge(prep, b + 1)
                nc.vector.tensor_tensor(key_f[:, b, :], key_f[:, b, :], typ_f[:, b, :], ALU.add).then_inc(keyed, 1)

            def look_for_strays():
                for b in range(BLOCKS):
                    if b >= 1:
                        dve.wait_ge(far_parts, 3 * b)
                    nc.vector.scalar_tensor_tensor(far_key[:, :], key_f[:, b, :], float(KEY_END), key_f[:, b, :],
                                                   ALU.is_lt, ALU.mult).then_inc(far_parts, 1)
                    nc.vector.tensor_reduce(lowest[:, b:b + 1], key_f[:, b, :], AX.X, ALU.min).then_inc(far_parts, 1)
                    dve.wait_ge(far_parts, 3 * b + 2)
                    nc.vector.tensor_reduce(highest[:, b:b + 1], far_key[:, :], AX.X, ALU.max).then_inc(far_parts, 1)
                dve.wait_ge(far_parts, 3 * BLOCKS)
                nc.vector.tensor_reduce(low_high[:, 0:1], lowest[:, :], AX.X, ALU.min).then_inc(far_parts, 1)
                nc.vector.tensor_reduce(low_high[:, 1:2], highest[:, :], AX.X, ALU.max).then_inc(far_parts, 1)
                dve.wait_ge(far_parts, 3 * BLOCKS + 2)
                nc.vector.tensor_scalar(far[:, :], low_high[:, 0:1], 0.0, None, ALU.is_lt).then_inc(far_parts, 1)
                dve.wait_ge(far_parts, 3 * BLOCKS + 3)
                nc.vector.scalar_tensor_tensor(far[:, :], low_high[:, 1:2], float(KEYS), far[:, :],
                                               ALU.is_ge, ALU.add).then_inc(far_counted, 1)

            def build_onehot(g, i):
                kt = key_t[:, bass.ds(g * CH, CH)]
                nc.vector.tensor_tensor(onehot[:, i, :, :], key_iota.unsqueeze(1).to_broadcast([P, CH, KEYS]),
                                        kt.unsqueeze(2).to_broadcast([P, CH, KEYS]), ALU.is_equal).then_inc(onehot_ready, 1)

            def add_window(g, at, quarter_n, half, i, first=False):
                base = dve.value_load(bases[0:1, bass.ds(g, 1)], min_val=0, max_val=N - 1)
                if not first:
                    dve.wait_ge(added, at)
                dve.wait_ge(h_ready, quarter_n + 1)
                window = acc[:, bass.ds(base, WIN)]
                nc.vector.tensor_tensor(window, window, p_h[half][:, i * WIN:(i + 1) * WIN], ALU.add).then_inc(added, 1)

            def add_quarter(k, q):
                for i in range(QUART):
                    s = q * QUART + i
                    add_window(k * TURN + (DENSE + s), pos(k, s), 4 * k + q, q % 2, i, is0(k) and s == 0)
                if q == 0 and not is0(k):
                    add_window(k - 1, pos_d(k), 4 * k, 0, QUART)

            def compare_nodes(k, n):
                j, c = n // PIECES, n % PIECES
                t0, t1 = CUTS[c], CUTS[c + 1]
                if c == 0:
                    dve.wait_ge(src_b_in[j % 2], ((k - 1) * 2 + (j // 2 + 1)) * 16)
                dve.wait_ge(node1h_used, k * (CH * PIECES) + (n - 1))
                nc.vector.tensor_tensor(node1h[:, n % 2, 0:t1 - t0, :],
                                        src_b[:, j % 2, :].unsqueeze(1).to_broadcast([P, t1 - t0, P]),
                                        tile_nodes[:, t0:t1].unsqueeze(2).to_broadcast([P, t1 - t0, P]),
                                        ALU.is_equal).then_inc(node1h_ready, 1)

            def build_rows(k, j):
                dve.wait_ge(node1h_used, k * (CH * PIECES) + (j + 1) * PIECES)
                dve.wait_ge(z_ready, pos_d(k) + 1)
                nc.vector.tensor_reduce(rows_d[:, j, :], p_turn[j % 2][:, 0:PARTS * D].rearrange("p (a d) -> p d a", a=PARTS),
                                        AX.X, ALU.add).then_inc(rows_built, 1)

            def quarter(k, q, dense=True, n=QUART):
                for i in range(n):
                    s = q * QUART + i
                    if not (is0(k) and q == 0):
                        before = pos(k, s - QUART) if q else pos(k - 1, s + TURN - QUART)
                        dve.wait_ge(z_ready, before + 1)
                    build_onehot(k * TURN + (DENSE + s), i)
                    if is0(k):
                        split(s)
                    elif dense:
                        for piece in SLOT_PIECES[s]:
                            compare_nodes(k, piece)
                        if q >= 1 and i == 1:
                            build_rows(k, q - 1)
                if q == 0 and not is0(k):
                    dve.wait_ge(z_ready, pos_d(k - 1) + 1)
                    build_onehot(k - 1, QUART)
                if not (is0(k) and q < 2):
                    add_quarter(*two_back(k, q))

            def split(s):
                i = s - 8
                if 0 <= i < SPLITS:
                    dve.wait_ge(x_hi, i + 1)
                    piece = x_f[:, i * ST:(i + 1) * ST, :]
                    nc.vector.tensor_tensor(piece, piece, x_parts[:, i * ST:(i + 1) * ST, 0, :], ALU.subtract).then_inc(x_less_hi, 1)
                i = s - 9
                if 0 <= i < SPLITS:
                    dve.wait_ge(x_mid, i + 1)
                    nc.vector.tensor_tensor(x_parts[:, i * ST:(i + 1) * ST, 2, :], x_f[:, i * ST:(i + 1) * ST, :],
                                            x_parts[:, i * ST:(i + 1) * ST, 1, :], ALU.subtract).then_inc(x_split, 1)

            dve.wait_ge(turned_out, 2)
            dve.wait_ge(const_in_psum, 2)
            quarter(0, 0)
            look_for_strays()
            dve.wait_ge(turned_out, 4 * BLOCKS)
            dve.wait_ge(far_counted, 1)
            nc.vector.memset(x_f[:, TILES - 1, :], 0.0).then_inc(x_pad, 1)
            nc.vector.memset(acc[:, :], 0.0).then_inc(acc_zero, 1)
            dve.wait_ge(acc_zero, 3)
            dve.wait_ge(bases_in, 32)
            for q in range(1, 4):
                quarter(0, q)
            dve.wait_ge(added, through(0, 1))
            for b in range(BATCHES):
                n = min(PER, TILES - b * PER) * P
                if b < BATCHES - 1:
                    dve.wait_ge(res_ready, b + 1)
                else:
                    dve.wait_ge(node1h_used, CH * PIECES)
                nodes = acc[:, b * BANK:b * BANK + n]
                last_add = nc.vector.tensor_tensor(nodes, nodes, p_turn[b % 2][:, 0:n], ALU.add)
                if b < BATCHES - 1:
                    last_add.then_inc(res_added, 1)
                else:
                    last_add.then_inc(rows_built, CH)
            dve.wait_ge(res_added, BATCHES - 1)
            dve.wait_ge(rows_built, CH)
            with dve.Fori(1, TURNS) as k:
                for q in range(4):
                    quarter(k, q)
                build_rows(k, CH - 1)
            for q in range(3):
                quarter(TURNS, q, dense=False)
            add_quarter(TURNS, 1)
            add_quarter(TURNS, 2)

            dve.wait_ge(added, GROUPS)
            dve.wait_ge(flag_ready, 1)
            with dve.If(dve.value_load(flag[0:1, 0:1]) > 0):
                nc.vector.tensor_scalar(outside, key_t[:, :], 0.0, None, ALU.is_lt).then_inc(st_keyed, 1)
                nc.vector.tensor_scalar(stray, typ_t[:, :], float(P), pid1[:, 0:1], ALU.mult, ALU.add).then_inc(st_keyed, 1)
                dve.wait_ge(st_keyed, 2)
                nc.vector.scalar_tensor_tensor(outside, key_t[:, :], float(KEYS), outside,
                                               ALU.is_ge, ALU.add).then_inc(st_keyed, 1)
                dve.wait_ge(st_keyed, 3)
                nc.vector.tensor_tensor(stray, stray, outside, ALU.mult).then_inc(st_keyed, 1)
                dve.wait_ge(st_keyed, 4)
                nc.vector.tensor_scalar(stray, stray, -1.0, None, ALU.add).then_inc(st_keyed, 1)
                dve.wait_ge(st_keyed, 5)

                def stray_group(g):
                    first = isinstance(g, int)
                    for j in range(CH):
                        if not (first and j == 0):
                            dve.wait_ge(st_z_ready, g * CH + j)
                        nc.vector.tensor_tensor(st_key1h, iota[:, :],
                                                stray[:, bass.ds(g * CH + j, 1)].to_broadcast([P, R * P]),
                                                ALU.is_equal).then_inc(st_onehot, 1)
                    if not first:
                        dve.wait_ge(st_added, g * NODE_WINS)
                        dve.wait_ge(st_dstep, g * NODE_WINS)
                    nc.vector.tensor_copy(st_dst[:, :], dst_t[:, bass.ds(g * CH, CH)]).then_inc(st_keyed, 1)
                    with dve.Fori(0, NODE_WINS) as w:
                        n = g * NODE_WINS + w
                        dve.wait_ge(st_keyed, g + 6)
                        nc.vector.tensor_tensor(st_dst1h,
                                                iota[:, 0:BANK].unsqueeze(1).to_broadcast([P, CH, BANK]),
                                                st_dst[:, :].unsqueeze(2).to_broadcast([P, CH, BANK]),
                                                ALU.is_equal).then_inc(st_win, 1)
                        dve.wait_ge(st_win, n + 1)
                        nc.vector.tensor_scalar(st_dst[:, :], st_dst[:, :], float(-BANK), None,
                                                ALU.add).then_inc(st_dstep, 1)
                        dve.wait_ge(st_dstep, n + 1)
                        dve.wait_ge(st_sum, n + 1)
                        nodes = acc[:, bass.ds(w * BANK, BANK)]
                        nc.vector.tensor_tensor(nodes, nodes, p_z[1][:, :], ALU.add).then_inc(st_added, 1)

                stray_group(0)
                with dve.Fori(1, GROUPS) as g:
                    stray_group(g)
                dve.wait_ge(st_added, GROUPS * NODE_WINS)

            def take_stats(b):
                tiles = range(b * PER, min(TILES, (b + 1) * PER))
                dve.wait_ge(y_ready, b + 1)
                for i, t in enumerate(tiles):
                    n = min(P, N - t * P)
                    nc.vector.bn_stats(stats[0:n, t, :], p_y[b % 4][0:n, i * D:(i + 1) * D]).then_inc(stats_taken, 1)
                for i, t in enumerate(tiles):
                    n = min(P, N - t * P)
                    dve.wait_ge(stats_taken, t + 1)
                    nc.vector.bn_aggr(mean_var[0:n, t, :], stats[0:n, t, :]).then_inc(aggregated, 1)

            def finish(b):
                t0, t1 = b * PER, min(TILES, (b + 1) * PER)
                n = min(P, N - t0 * P)
                dve.wait_ge(std_known, b + 1)
                nc.vector.reciprocal(rstd[0:n, t0:t1], std[0:n, t0:t1]).then_inc(rstd_known, 1)
                dve.wait_ge(rstd_known, b + 1)
                nc.vector.scalar_tensor_tensor(shift[0:n, t0:t1], mean_var[0:n, t0:t1, 0], -1.0, rstd[0:n, t0:t1],
                                               ALU.mult, ALU.mult).then_inc(norm_known, 1)

            for b in range(BATCHES):
                take_stats(b)
                if b >= 1:
                    finish(b - 1)
            finish(BATCHES - 1)

        @block.tensor
        def _(pe):
            pe.wait_ge(ident_ready, 2)
            for b in range(BLOCKS):
                for q, listed in enumerate((src_f, key_f, typ_f, dst_f)):
                    n = 4 * b + q
                    if q == 0:
                        pe.wait_ge(src_cast, b + 1)
                    if q == 1:
                        pe.wait_ge(keyed, b + 1)
                    if n >= 2:
                        pe.wait_ge(turned_out, n - 1)
                    for j in range(CH):
                        last = nc.tensor.transpose(p_turn[n % 2][:, j * P:(j + 1) * P], listed[:, b, j * P:(j + 1) * P],
                                                   ident[:, :])
                    last.then_inc(turned, 1)

            def sums(k, s):
                at = pos(k, s)
                pe.wait_ge(landed[s % SLOTS], (k * 2 + (s // SLOTS + 1)) * (16 * CH))
                pe.wait_ge(onehot_ready, at + 1)
                if not (is0(k) and s < 2):
                    pe.wait_ge(z_copied, (pos(k, s - 2) if s >= 2 else pos(k - 1, s + TURN - 2)) + 1)
                for j in range(CH):
                    last = nc.tensor.matmul(p_z[s % 2][:, 0:KEYS], rows[:, s % SLOTS, j, :], onehot[:, s % QUART, j, :],
                                            start=(j == 0), stop=(j == CH - 1))
                last.then_inc(z_ready, 1)

            def sums_dense(k):
                pe.wait_ge(landed_d, 16 * CH)
                pe.wait_ge(rows_built, k * CH)
                pe.wait_ge(onehot_ready, pos_d(k) + 1)
                pe.wait_ge(z_copied, pos_d(k - 1) + 1)
                for j in range(CH):
                    last = nc.tensor.matmul(p_zd, rows_d[:, j, :], onehot[:, QUART, j, :],
                                            start=(j == 0), stop=(j == CH - 1))
                last.then_inc(z_ready, 1)

            def products(k, q):
                n = QUART + (q == 0 and not is0(k))
                pe.wait_ge(z_copied, through(k, q))
                if not (is0(k) and q < 2):
                    pe.wait_ge(added, through(*two_back(k, q)))
                for r in range(R):
                    last = nc.tensor.matmul(p_h[q % 2][:, 0:n * WIN], W_sb[:, r, :],
                                            z_sb[:, q % 2, r, 0:n, :].rearrange("p i d -> p (i d)"),
                                            start=(r == 0), stop=(r == R - 1))
                last.then_inc(h_ready, 1)

            def dense_piece(k, n):
                j, c = n // PIECES, n % PIECES
                at = (k - 1) * (CH * PIECES) + n
                pe.wait_ge(node1h_ready, at + 1)
                if c == 0:
                    if j < 2:
                        pe.wait_ge(res_added, BATCHES - 1)
                    pe.wait_ge(rows_built, k * CH + (j - 1))
                for t in range(CUTS[c], CUTS[c + 1]):
                    last = nc.tensor.matmul(p_turn[j % 2][:, 0:PARTS * D], node1h[:, n % 2, t - CUTS[c], :],
                                            x_parts[:, t, :, :].rearrange("p a d -> p (a d)"),
                                            start=(t == 0), stop=(t == TILES - 1))
                last.then_inc(node1h_used, 1)

            def turn(k, quarters=4, dense=True):
                for q in range(quarters):
                    for s in range(q * QUART, (q + 1) * QUART):
                        sums(k, s)
                        if s == QUART - 1 and not is0(k):
                            sums_dense(k)
                        if dense and not is0(k):
                            for piece in SLOT_PIECES[s]:
                                dense_piece(k, piece)
                    if q >= 1:
                        products(k, q - 1)
                    elif not is0(k):
                        products(k - 1, 3)

            pe.wait_ge(w_in, 16)
            turn(0)
            pe.wait_ge(x_split, SPLITS)
            for b in range(BATCHES):
                if b >= 2:
                    pe.wait_ge(res_added, b - 1)
                for i in range(min(PER, TILES - b * PER)):
                    for a in range(PARTS):
                        last = nc.tensor.matmul(p_turn[b % 2][:, i * P:(i + 1) * P], x_parts[:, b * PER + i, a, :],
                                                ident2[:, :], start=(a == 0), stop=(a == PARTS - 1))
                if b < BATCHES - 1:
                    last.then_inc(res_ready, 1)
                else:
                    last.then_inc(node1h_used, CH * PIECES)
            with pe.Fori(1, TURNS) as k:
                turn(k)
            turn(TURNS, quarters=3, dense=False)
            products(TURNS, 2)

            pe.wait_ge(far_counted, 1)
            pe.wait_ge(const_in_psum, 2)
            nc.tensor.matmul(p_flag, far[:, :], ones[:, :], start=True, stop=True).then_inc(far_summed, 1)

            pe.wait_ge(flag_ready, 1)
            with pe.If(pe.value_load(flag[0:1, 0:1]) > 0):
                def stray_group(g):
                    pe.wait_ge(st_landed, (g + 1) * (16 * CH))
                    for j in range(CH):
                        pe.wait_ge(st_onehot, g * CH + (j + 1))
                        for h in range(2):
                            last = nc.tensor.matmul(p_turn[h][:, :], rows[:, 0, j, :], st_key1h[:, h * BANK:(h + 1) * BANK],
                                                    start=True, stop=True)
                        last.then_inc(st_z_ready, 1)
                        pe.wait_ge(st_z_copied, g * CH + (j + 1))
                        if j >= 1:
                            pe.wait_ge(st_m_copied, g * CH + j)
                        for r in range(R):
                            last = nc.tensor.matmul(p_z[0][:, 0:D], st_z[:, r, :], W_sb[:, r, :],
                                                    start=(r == 0), stop=(r == R - 1))
                        last.then_inc(st_m_ready, 1)
                    with pe.Fori(0, NODE_WINS) as w:
                        pe.wait_ge(st_m_copied, (g + 1) * CH)
                        pe.wait_ge(st_win, g * NODE_WINS + w + 1)
                        for j in range(CH):
                            last = nc.tensor.matmul(p_z[1][:, :], st_msg[:, j, :], st_dst1h[:, j, :],
                                                    start=(j == 0), stop=(j == CH - 1))
                        last.then_inc(st_sum, 1)

                stray_group(0)
                with pe.Fori(1, GROUPS) as g:
                    stray_group(g)
                pe.wait_ge(st_added, GROUPS * NODE_WINS)

            pe.wait_ge(added, GROUPS)
            for b in range(BATCHES):
                if b >= 4:
                    pe.wait_ge(normed, (b - 3) * PER)
                for i in range(min(PER, TILES - b * PER)):
                    t = b * PER + i
                    n = min(P, N - t * P)
                    last = nc.tensor.transpose(p_y[b % 4][0:n, i * D:(i + 1) * D], acc[:, t * P:t * P + n], ident[:, :])
                last.then_inc(y_ready, 1)


def kernel(x, src, dst, edge_type_8, L0_gnn_W):
    import numpy as np
    import concourse.bacc as bacc
    from concourse.bass_utils import run_bass_kernel_spmd

    nc = bacc.Bacc("TRN2", target_bir_lowering=False, num_devices=1)
    arrays, args = {}, []
    for name, a in (("x", x), ("src", src), ("dst", dst), ("edge_type", edge_type_8), ("W", L0_gnn_W)):
        a = np.ascontiguousarray(a)
        arrays[f"in_{name}"] = a
        args.append(nc.dram_tensor(f"in_{name}", a.shape, mybir.dt.from_np(a.dtype), kind="ExternalInput").ap())
    args.append(nc.dram_tensor("out_0", arrays["in_x"].shape, FP32, kind="ExternalOutput").ap())
    build(nc, *args)
    return run_bass_kernel_spmd(nc, [arrays], core_ids=[0]).results[0]["out_0"]
```

```python
import concourse.bass as bass
from concourse import mybir
from contextlib import ExitStack

FP32 = mybir.dt.float32
BF16 = mybir.dt.bfloat16
FP16 = mybir.dt.float16
I32 = mybir.dt.int32
I16 = mybir.dt.int16
ALU = mybir.AluOpType
ACT = mybir.ActivationFunctionType
AX = mybir.AxisListType

EPS = 1e-5
P = 128
CH = 4
GE = CH * P
WIN = 22
SLOTS = 5
TURN = 10
LOT = 5
LOTS = TURN // LOT
HALF = 3
DAT = 1
PARTS = 3
BANK = 512
FIRST, STEP = 4, 10
EARLY_LO, EARLY_HI = 2, 11
EARLY_AT = {1: 1, 2: 3, 3: 3, 4: 2}
PAD_DST = 32767


def build(nc, x, src, dst, etype, W, out):
    N, D = x.shape
    E = src.shape[0]
    R = W.shape[0]
    KEYS = WIN * R
    GROUPS = -(-E // GE)
    BLOCKS = -(-GROUPS // P)
    FULL = E // GE - (BLOCKS - 1) * P
    TAIL = E - (E // GE) * GE
    TURNS = (GROUPS - LOT - 1) // (TURN + 1)
    DENSE = TURNS
    GATHERED = GROUPS - DENSE
    REST = GATHERED - TURNS * TURN
    ROUNDS = GATHERED // SLOTS
    REST_SLOTS = GATHERED - ROUNDS * SLOTS
    REST_LOTS = [min(LOT, REST - n) for n in range(0, REST, LOT)]
    assert TURNS * TURN + SLOTS <= GATHERED
    assert len(REST_LOTS) >= 2 and REST_SLOTS > 0 and TAIL > 0 and LOTS % 2 == 0
    NODE_WINS = -(-N // BANK)
    ACC = NODE_WINS * BANK
    TILES = -(-N // P)
    LAST = N - (TILES - 1) * P
    PER = BANK // D
    BATCHES = -(-TILES // PER)
    EARLY = EARLY_HI - EARLY_LO
    REDO = EARLY + EARLY_LO
    ORDER = list(range(EARLY_LO, EARLY_HI)) + list(range(EARLY_LO)) + list(range(EARLY_HI, BATCHES))
    ORDER += ORDER[:REDO]
    assert EARLY == sum(EARLY_AT.values()) and max(EARLY_AT) < min(REST, LOT) and EARLY_HI < BATCHES
    SPLITS = 7
    ST = TILES // SPLITS
    BATCHES_AT = 4
    STEPS = -(-BATCHES // BATCHES_AT)
    assert STEPS < TURN - LOT + 1 and LOTS == 2 and ACC >= N + WIN and ST * SPLITS == TILES
    KEY_END = R * N
    assert (PAD_DST - N) * R > KEY_END and PAD_DST >= ACC
    CUTS = [n // 2 * STEP + n % 2 * FIRST for n in range(TURN)] + [TILES]
    PIECES = len(CUTS) - 1
    PAIRS = -(-TILES // 2)
    WIDE = max(b - a for a, b in zip(CUTS, CUTS[1:]))
    assert PIECES % 2 == 0 and all(c % 2 == 0 for c in CUTS[:-1]) and min(b - a for a, b in zip(CUTS, CUTS[1:])) > 0
    assert 2 * KEYS <= BANK
    F32_TURNS = 2
    F32_ROUNDS = F32_TURNS * TURN // SLOTS
    ROW = PARTS * D
    x_table = nc.dram_tensor("x_table", [TILES * P, ROW], BF16).ap()

    ctx = ExitStack()
    with ctx:
        def sb(name, shape, dt=FP32):
            return ctx.enter_context(nc.sbuf_tensor(name, shape, dt))

        def ps(name):
            return ctx.enter_context(nc.psum_tensor(name, [P, BANK], FP32))

        def sem(name):
            return ctx.enter_context(nc.semaphore(name))

        acc = sb("acc", [D, ACC])
        raw = acc[:, 0:3 * BLOCKS * GE].bitcast(I32).rearrange("p (l b e) -> p l b e", l=3, b=BLOCKS)
        src_raw, dst_raw, typ_raw = (raw[:, i, :, :] for i in range(3))
        stage = sb("stage", [P, 4 * BLOCKS * GE])
        lists_f = stage[:, :].rearrange("p (l b e) -> p l b e", l=4, b=BLOCKS)
        src_f, key_f, typ_f, dst_f = (lists_f[:, i, :, :] for i in range(4))
        x_f = stage[:, 0:TILES * D].rearrange("p (t d) -> p t d", d=D)
        COLS = BLOCKS * P * CH
        stray = stage[:, 0:COLS]
        outside = stage[:, COLS:2 * COLS]
        st_dst1h = stage[:, COLS:COLS + CH * BANK].rearrange("p (j n) -> p j n", j=CH)
        st_key1h = stage[:, 2 * COLS:2 * COLS + R * P]
        st_z = stage[:, 2 * COLS + R * P:2 * COLS + 2 * R * P].rearrange("p (r e) -> p r e", r=R)
        st_msg = stage[:, 2 * COLS + 2 * R * P:2 * COLS + 2 * R * P + CH * D].rearrange("p (j d) -> p j d", j=CH)
        y = stage[:, 0:4 * PER * D].rearrange("p (b i d) -> p b i d", b=4, i=PER)
        src_t = sb("src_t", [P, COLS], I16)
        key_t = sb("key_t", [P, COLS])
        typ_t = sb("typ_t", [P, COLS], I16)
        dst_t = sb("dst_t", [P, COLS], I16)
        bases = sb("bases", [1, GROUPS], I32)
        W_sb = sb("W_sb", [D, R, D])
        x_parts = sb("x_parts", [P, TILES, PARTS, D], BF16)
        iota = sb("iota", [P, R * P])
        tile_base = sb("tile_base", [P, TILES])
        pid = sb("pid", [P, 1])
        pid1 = sb("pid1", [P, 1])
        ident = sb("ident", [P, P])
        ones = sb("ones", [P, 1])
        src_slot = sb("src_slot", [P, SLOTS + 1, CH], I32)
        rows_b = sb("rows_b", [P, SLOTS, CH, ROW], BF16)
        rows = rows_b[:, :, :, :].bitcast(FP32)[:, :, :, 0:D]
        rows_0 = sb("rows_0", [P, CH, D])
        onehot = sb("onehot", [P, LOT, CH, KEYS])
        onehot_b = onehot[:, :, :, :].bitcast(BF16)[:, :, :, 0:KEYS]
        onehot_0 = sb("onehot_0", [P, CH, KEYS])
        onehot_d = sb("onehot_d", [P, CH, KEYS], BF16)
        src_rel = sb("src_rel", [P, CH, TILES])
        node1h = sb("node1h", [P, 2, CH, WIDE, P], BF16)
        counts = sb("counts", [P, 2, 2 * KEYS], FP16)
        z_sb = sb("z_sb", [D, 2, R, LOT + 1, WIN])
        far_key = sb("far_key", [P, GE])
        lowest = sb("lowest", [P, BLOCKS])
        highest = sb("highest", [P, BLOCKS])
        low_high = sb("low_high", [P, 2])
        far = sb("far", [P, 2])
        misplaced = sb("misplaced", [1, REST + 1])
        n_misplaced = sb("n_misplaced", [1, 1])
        flag = sb("flag", [1, 4], I32)
        stats = sb("stats", [P, TILES, 6])
        mean_var = sb("mean_var", [P, BATCHES * PER, 2])
        eps = sb("eps", [P, 1])
        std = sb("std", [P, BATCHES * PER])
        rstd = sb("rstd", [P, BATCHES * PER])
        shift = sb("shift", [P, BATCHES * PER])
        st_dst = sb("st_dst", [P, CH])

        p_iota = ps("p_iota")
        p_turn = [ps("p_turn0"), ps("p_turn1")]
        p_z = [ps("p_z0"), ps("p_z1")]
        p_dense = ps("p_dense")
        p_zd = p_dense[:, 0:KEYS]
        p_h = [ps("p_h0"), ps("p_h1")]
        p_flag = p_turn[0][0:1, 0:2]
        p_y = [p_turn[0], p_turn[1], p_dense, p_iota]

        src_in = [sem(f"src_in{b}") for b in range(BLOCKS)]
        dst_typ_in = [sem(f"dst_typ_in{b}") for b in range(BLOCKS)]
        bases_in = sem("bases_in")
        w_in = sem("w_in")
        x_in = sem("x_in")
        pads_set = sem("pads_set")
        small_set = sem("small_set")
        acc_set = sem("acc_set")
        iota_ready = sem("iota_ready")
        const_in_psum = sem("const_in_psum")
        ident_ready = sem("ident_ready")
        src_cast = sem("src_cast")
        lists_cast = sem("lists_cast")
        keyed = sem("keyed")
        prep = sem("prep")
        turned = sem("turned")
        turned_out = sem("turned_out")
        base_parts = sem("base_parts")
        far_parts = sem("far_parts")
        far_counted = sem("far_counted")
        far_summed = sem("far_summed")
        flag_ready = sem("flag_ready")
        x_pad = sem("x_pad")
        x_hi = sem("x_hi")
        x_less_hi = sem("x_less_hi")
        x_mid = sem("x_mid")
        x_split = sem("x_split")
        table_stored = sem("table_stored")
        x_turned = sem("x_turned")
        landed = [sem(f"landed{s}") for s in range(SLOTS)]
        landed_0 = sem("landed_0")
        first_idx = sem("first_idx")
        idx_ready = [sem(f"idx_ready{s}") for s in range(SLOTS)]
        onehot_ready = sem("onehot_ready")
        z_ready = sem("z_ready")
        z_copied = sem("z_copied")
        h_ready = sem("h_ready")
        added = sem("added")
        node1h_ready = sem("node1h_ready")
        onehot_0_ready = sem("onehot_0_ready")
        src_rel_ready = sem("src_rel_ready")
        onehot_d_ready = sem("onehot_d_ready")
        counts_ready = sem("counts_ready")
        counts_copied = sem("counts_copied")
        st_keyed = sem("st_keyed")
        st_idx = sem("st_idx")
        st_landed = sem("st_landed")
        st_onehot = sem("st_onehot")
        st_z_ready = sem("st_z_ready")
        st_z_copied = sem("st_z_copied")
        st_m_ready = sem("st_m_ready")
        st_m_copied = sem("st_m_copied")
        st_dstep = sem("st_dstep")
        st_win = sem("st_win")
        st_sum = sem("st_sum")
        st_added = sem("st_added")
        y_ready = sem("y_ready")
        aggregated = sem("aggregated")
        norm_known = sem("norm_known")
        std_known = sem("std_known")
        rstd_known = sem("rstd_known")
        stats_taken = sem("stats_taken")
        normed = sem("normed")
        stored = [sem(f"stored{i}") for i in range(4)]

        def is0(k):
            return isinstance(k, int) and k == 0

        def pos(k, s):
            return s if is0(k) else k * (TURN + 1) + (s - 1 + (s >= DAT))

        def pos_d(k):
            return k * (TURN + 1) + (DAT - 1)

        def pairs_through(n):
            return -(-CUTS[n + 1] // 2)

        def pairs_of(n):
            return range(CUTS[n] // 2, pairs_through(n))

        def through(k, q, n=LOT):
            return k * (TURN + 1) + (LOT * q + n)

        def two_back(k, q):
            return (k, q - 2) if q >= 2 else (k - 1, q + LOTS - 2)

        def follows_dense(k):
            return not (isinstance(k, int) and k < 2)

        def is_f32(k):
            return isinstance(k, int) and k < F32_TURNS

        def in_first_lots(k, q):
            return is0(k) and q < 2

        def early_at(s):
            n = sum(EARLY_AT.get(i, 0) for i in range(s))
            return range(n, n + EARLY_AT.get(s, 0))

        def splits_at(n):
            a, b = (min(TILES, m * BATCHES_AT * PER) // ST for m in (n, n + 1))
            return range(a, b) if n >= 0 else range(0)

        def batches_at(n):
            return range(n * BATCHES_AT, min(BATCHES, (n + 1) * BATCHES_AT)) if n >= 0 else range(0)

        def tiles_of(n):
            return range(ORDER[n] * PER, min(TILES, (ORDER[n] + 1) * PER))

        def tiles_through(n):
            return sum(len(tiles_of(m)) for m in range(n + 1))

        def n_stores(i, upto):
            k = 0
            for n in range(i, upto, 4):
                t0, t1 = tiles_of(n)[0], tiles_of(n)[-1] + 1
                whole = min(t1, N // P)
                k += (whole > t0) + (whole < t1)
            return k

        block = ctx.enter_context(nc.Block())

        @block.sync
        def _(sp):
            def load(dram, into, b, done):
                n = P if b < BLOCKS - 1 else FULL
                e0 = b * P * GE
                sp.dma_start(into[0:n, b, :], dram[e0:e0 + n * GE].rearrange("(g e) -> g e", e=GE)).then_inc(done, 16)
                if b == BLOCKS - 1:
                    sp.dma_start(into[n:n + 1, b, 0:TAIL],
                                 dram[e0 + n * GE:E].rearrange("(g e) -> g e", g=1)).then_inc(done, 16)

            sp.dma_start(src_slot[:, 0:SLOTS, :],
                         src[DENSE * GE:(DENSE + SLOTS) * GE].rearrange("(g p j) -> p g j", p=P, j=CH)).then_inc(first_idx, 16)
            sp.dma_start(src_slot[:, SLOTS, :], src[0:GE].rearrange("(p j) -> p j", j=CH)).then_inc(first_idx, 16)
            load(src, src_raw, 0, src_in[0])
            load(dst, dst_raw, 0, dst_typ_in[0])
            load(etype, typ_raw, 0, dst_typ_in[0])
            sp.wait_ge(pads_set, 3)
            for b in range(1, BLOCKS):
                load(src, src_raw, b, src_in[b])
                load(dst, dst_raw, b, dst_typ_in[b])
                load(etype, typ_raw, b, dst_typ_in[b])
            sp.dma_start(bases[0:1, 0:GROUPS - 1],
                         dst[0:(GROUPS - 1) * GE].rearrange("(o g e) -> o g e", o=1, e=GE)[:, :, 0],
                         allow_slow_non_contiguous=True).then_inc(bases_in, 16)
            sp.dma_start(bases[0:1, GROUPS - 1:GROUPS],
                         dst[(GROUPS - 1) * GE:(GROUPS - 1) * GE + 1].rearrange("(o g) -> o g", o=1)).then_inc(bases_in, 16)
            sp.dma_start(W_sb[:, :, :], W.rearrange("r i o -> i r o")).then_inc(w_in, 16)
            sp.wait_ge(x_pad, 1)
            sp.dma_start(x_f[:, 0:TILES - 1, :],
                         x[0:(TILES - 1) * P, :].rearrange("(t p) d -> p t d", p=P)).then_inc(x_in, 16)
            sp.dma_start(x_f[0:LAST, TILES - 1, :], x[(TILES - 1) * P:N, :]).then_inc(x_in, 16)

            for i in range(SPLITS):
                sp.wait_ge(x_split, i + 1)
                sp.dma_start(x_table[i * ST * P:(i + 1) * ST * P, :].rearrange("(t p) c -> p t c", p=P),
                             x_parts[:, i * ST:(i + 1) * ST, :, :].rearrange("p t a d -> p t (a d)")
                             ).then_inc(table_stored, 16)

            def store(n):
                t0, t1 = tiles_of(n)[0], tiles_of(n)[-1] + 1
                whole = min(t1, N // P)
                sp.wait_ge(normed, tiles_through(n))
                if whole > t0:
                    sp.dma_start(out[t0 * P:whole * P, :].rearrange("(t p) d -> p t d", p=P),
                                 y[:, n % 4, 0:whole - t0, :]).then_inc(stored[n % 4], 16)
                if whole < t1:
                    sp.dma_start(out[whole * P:N, :], y[0:N - whole * P, n % 4, whole - t0, :]).then_inc(stored[n % 4], 16)

            sp.wait_ge(flag_ready, 1)
            redo = sp.value_load(flag[0:1, 1:2])
            for n in range(BATCHES):
                store(n)
            for i in range(4):
                sp.wait_ge(stored[i], 16 * n_stores(i, BATCHES))
            with sp.If(redo > 0):
                for n in range(BATCHES, BATCHES + REDO):
                    store(n)
                for i in range(4):
                    sp.wait_ge(stored[i], 16 * n_stores(i, BATCHES + REDO))

        @block.gpsimd
        def _(pool):
            pool.iota(iota[:, :], [[1, R * P]], base=0, channel_multiplier=0,
                      allow_small_or_imprecise_dtypes=True).then_inc(iota_ready, 1)
            pool.iota(pid[:, :], [[1, 1]], base=0, channel_multiplier=1,
                      allow_small_or_imprecise_dtypes=True).then_inc(iota_ready, 1)
            pool.iota(pid1[:, :], [[1, 1]], base=1, channel_multiplier=1,
                      allow_small_or_imprecise_dtypes=True).then_inc(iota_ready, 1)
            pool.iota(tile_base[:, :], [[P, TILES]], base=0, channel_multiplier=0,
                      allow_small_or_imprecise_dtypes=True).then_inc(iota_ready, 1)

            def gather(slot, done, into=None, table=x_table):
                if into is None:
                    into = rows_b[:, slot, :, :]
                for j in range(CH):
                    pool.indirect_dma_start(into[:, j, :], None, table[:, :],
                                            bass.IndirectOffsetOnAxis(ap=src_slot[:, slot, j:j + 1], axis=0)).then_inc(done, 16)

            pool.wait_ge(first_idx, 32)
            for s in range(SLOTS):
                gather(s, landed[s], rows[:, s, :, :], x)
            gather(SLOTS, landed_0, rows_0, x)
            with pool.Fori(1, F32_ROUNDS) as k:
                for s in range(SLOTS):
                    pool.wait_ge(turned_out, 1)
                    pool.wait_ge(idx_ready[s], k)
                    gather(s, landed[s], rows[:, s, :, :], x)
            pool.wait_ge(table_stored, 16 * SPLITS)
            with pool.Fori(F32_ROUNDS, ROUNDS) as k:
                for s in range(SLOTS):
                    pool.wait_ge(turned_out, 1)
                    pool.wait_ge(idx_ready[s], k)
                    gather(s, landed[s])
            for s in range(REST_SLOTS):
                pool.wait_ge(idx_ready[s], ROUNDS)
                gather(s, landed[s])

            pool.wait_ge(flag_ready, 1)
            with pool.If(pool.value_load(flag[0:1, 0:1]) > 0):
                with pool.Fori(1, GROUPS + 1) as g1:
                    pool.wait_ge(turned_out, 1)
                    pool.wait_ge(st_idx, g1)
                    gather(0, st_landed, rows[:, 0, :, :], x)

        @block.scalar
        def _(act):
            for b in range(BLOCKS):
                act.wait_ge(src_in[b], 16 if b < BLOCKS - 1 else 32)
                nc.scalar.copy(src_f[:, b, :], src_raw[:, b, :]).then_inc(src_cast, 1)
                for q, table in enumerate((src_t, key_t, typ_t, dst_t)):
                    n = 4 * b + q
                    act.wait_ge(turned, n + 1)
                    turned_list = p_turn[n % 2][:, :].rearrange("p (j g) -> p g j", j=CH)
                    nc.scalar.copy(table[:, b * GE:(b + 1) * GE].rearrange("p (g j) -> p g j", j=CH),
                                   turned_list).then_inc(turned_out, 1)
                    if n == 0:
                        act.wait_ge(iota_ready, 4)
                        nc.scalar.copy(p_iota[:, 0:KEYS], iota[:, 0:KEYS]).then_inc(const_in_psum, 1)

            def copy_counts(k, c):
                act.wait_ge(counts_ready, (k - 1) * PAIRS + (c + 1))
                n = min(2, TILES - 2 * c) * KEYS
                nc.scalar.copy(counts[:, c % 2, 0:n], p_turn[c % 2][:, 0:n]).then_inc(counts_copied, 1)

            def copy_lot(k, q, n=LOT, refill=LOT, dense=True, after=None):
                for i in range(n):
                    s = q * LOT + i
                    act.wait_ge(z_ready, pos(k, s) + 1)
                    if i == 0 and not in_first_lots(k, q):
                        act.wait_ge(h_ready, LOTS * k + (q - 1))
                    nc.scalar.copy(z_sb[:, q % 2, :, i, :],
                                   p_z[s % 2][:, 0:KEYS].rearrange("p (d r) -> p r d", r=R)).then_inc(z_copied, 1)
                    if i < refill:
                        g = k * TURN + (DENSE + s + SLOTS)
                        nc.scalar.copy(src_slot[:, s % SLOTS, :], src_t[:, bass.ds(g * CH, CH)]
                                       ).then_inc(idx_ready[s % SLOTS], 1)
                    if is0(k):
                        split(s)
                    elif s == DAT - 1:
                        act.wait_ge(z_ready, pos_d(k) + 1)
                        nc.scalar.copy(z_sb[:, 0, :, LOT, :],
                                       p_zd.rearrange("p (d r) -> p r d", r=R)).then_inc(z_copied, 1)
                    if dense:
                        for c in pairs_of(s):
                            copy_counts(k, c)
                    if after:
                        after(s)

            def split(s):
                for b in batches_at(s - LOT):
                    n = min(PER, TILES - b * PER) * P
                    act.wait_ge(x_turned, b + 1)
                    nc.scalar.activation(acc[:, b * BANK:b * BANK + n], p_turn[b % 2][:, 0:n], ACT.Identity,
                                         scale=2.0).then_inc(acc_set, 1)
                for i in splits_at(s - LOT):
                    act.wait_ge(x_in, 32)
                    nc.scalar.copy(x_parts[:, i * ST:(i + 1) * ST, 0, :], x_f[:, i * ST:(i + 1) * ST, :]).then_inc(x_hi, 1)
                for i in splits_at(s - LOT - 1):
                    act.wait_ge(x_less_hi, i + 1)
                    nc.scalar.copy(x_parts[:, i * ST:(i + 1) * ST, 1, :], x_f[:, i * ST:(i + 1) * ST, :]).then_inc(x_mid, 1)

            for q in range(LOTS):
                copy_lot(0, q, dense=False)
            split(TURN)
            act.wait_ge(far_summed, 1)
            nc.scalar.copy(flag[0:1, 0:2], p_flag).then_inc(flag_ready, 1)
            for q in range(LOTS):
                copy_lot(1, q)
            with act.Fori(2, TURNS) as k:
                for q in range(LOTS):
                    copy_lot(k, q)
            act.wait_ge(flag_ready, 1)
            strays = act.value_load(flag[0:1, 0:1])
            redo = act.value_load(flag[0:1, 1:2])

            def deviations(n):
                t0, t1 = tiles_of(n)[0], tiles_of(n)[-1] + 1
                m = min(P, N - t0 * P)
                act.wait_ge(aggregated, tiles_through(n))
                nc.scalar.activation(std[0:m, t0:t1], mean_var[0:m, t0:t1, 1], ACT.Sqrt,
                                     bias=eps[0:m, 0:1], scale=1.0).then_inc(std_known, 1)

            def normalise(n):
                act.wait_ge(norm_known, n + 1)
                if n >= 4:
                    act.wait_ge(stored[n % 4], 16 * n_stores(n % 4, n))
                for i, t in enumerate(tiles_of(n)):
                    m = min(P, N - t * P)
                    nc.scalar.activation(y[0:m, n % 4, i, :], p_y[n % 4][0:m, i * D:(i + 1) * D], ACT.Identity,
                                         bias=shift[0:m, t:t + 1], scale=rstd[0:m, t:t + 1]).then_inc(normed, 1)

            def normalise_early(s):
                for n in early_at(s):
                    deviations(n)
                    if n > 0:
                        normalise(n - 1)
                    if n == EARLY - 1:
                        normalise(n)

            for q, n in enumerate(REST_LOTS):
                copy_lot(TURNS, q, n, refill=max(0, min(LOT, GATHERED - SLOTS - TURNS * TURN - q * LOT)), dense=False,
                         after=normalise_early)

            for n in range(EARLY, REDO):
                deviations(n)
            for n in range(EARLY, REDO):
                normalise(n)

            with act.If(strays > 0):
                def stray_group(g):
                    if not isinstance(g, int):
                        act.wait_ge(st_z_ready, g * CH)
                    nc.scalar.copy(src_slot[:, 0, :], src_t[:, bass.ds(g * CH, CH)]).then_inc(st_idx, 1)
                    for j in range(CH):
                        act.wait_ge(st_z_ready, g * CH + (j + 1))
                        for h in range(2):
                            last = nc.scalar.copy(st_z[:, 4 * h:4 * h + 4, :],
                                                  p_turn[h][:, :].rearrange("p (r e) -> p r e", e=P))
                        last.then_inc(st_z_copied, 1)
                        act.wait_ge(st_m_ready, g * CH + (j + 1))
                        nc.scalar.copy(st_msg[:, j, :], p_z[0][:, 0:D]).then_inc(st_m_copied, 1)

                stray_group(0)
                with act.Fori(1, GROUPS) as g:
                    stray_group(g)

            for n in range(REDO, BATCHES):
                deviations(n)
                if n > REDO:
                    normalise(n - 1)
            normalise(BATCHES - 1)
            with act.If(redo > 0):
                for n in range(BATCHES, BATCHES + REDO):
                    deviations(n)
                    normalise(n)

        @block.vector
        def _(dve):
            last = BLOCKS - 1
            nc.vector.memset(src_raw[:, last, :], 0).then_inc(pads_set, 1)
            nc.vector.memset(dst_raw[:, last, :], PAD_DST).then_inc(pads_set, 1)
            nc.vector.memset(typ_raw[:, last, :], 0).then_inc(pads_set, 1)
            nc.vector.memset(ones[:, :], 1.0).then_inc(small_set, 1)
            nc.vector.memset(eps[:, :], EPS).then_inc(small_set, 1)
            dve.wait_ge(iota_ready, 4)
            nc.vector.tensor_scalar(ident[:, :], iota[:, 0:P], pid[:, 0:1], None, ALU.is_equal).then_inc(ident_ready, 1)
            for b in range(BLOCKS):
                dve.wait_ge(dst_typ_in[b], 32 if b < last else 64)
                nc.vector.tensor_copy(dst_f[:, b, :], dst_raw[:, b, :]).then_inc(lists_cast, 1)
                nc.vector.tensor_copy(typ_f[:, b, :], typ_raw[:, b, :]).then_inc(lists_cast, 1)
                dve.wait_ge(lists_cast, 2 * b + 2)
                nc.vector.tensor_scalar(key_f[:, b, :], dst_f[:, b, :], dst_f[:, b, 0:1], float(R),
                                        ALU.subtract, ALU.mult).then_inc(prep, 1)
                dve.wait_ge(prep, b + 1)
                nc.vector.tensor_tensor(key_f[:, b, :], key_f[:, b, :], typ_f[:, b, :], ALU.add).then_inc(keyed, 1)

            def look_for_strays():
                nc.vector.tensor_scalar(misplaced[:, 0:REST], bases[:, GROUPS - REST:GROUPS], float(EARLY_HI * PER * P), None,
                                        ALU.is_lt).then_inc(base_parts, 1)
                nc.vector.tensor_scalar(misplaced[:, REST:REST + 1], bases[:, DENSE - 1:DENSE],
                                        float(EARLY_LO * PER * P - WIN), None, ALU.is_gt).then_inc(base_parts, 1)
                dve.wait_ge(base_parts, 2)
                nc.vector.tensor_reduce(n_misplaced[:, :], misplaced[:, :], AX.X, ALU.add).then_inc(base_parts, 1)
                for b in range(BLOCKS):
                    if b >= 1:
                        dve.wait_ge(far_parts, 3 * b)
                    nc.vector.scalar_tensor_tensor(far_key[:, :], key_t[:, b * GE:(b + 1) * GE], float(KEY_END), key_t[:, b * GE:(b + 1) * GE],
                                                   ALU.is_lt, ALU.mult).then_inc(far_parts, 1)
                    nc.vector.tensor_reduce(lowest[:, b:b + 1], key_t[:, b * GE:(b + 1) * GE], AX.X, ALU.min).then_inc(far_parts, 1)
                    dve.wait_ge(far_parts, 3 * b + 2)
                    nc.vector.tensor_reduce(highest[:, b:b + 1], far_key[:, :], AX.X, ALU.max).then_inc(far_parts, 1)
                dve.wait_ge(far_parts, 3 * BLOCKS)
                nc.vector.tensor_reduce(low_high[:, 0:1], lowest[:, :], AX.X, ALU.min).then_inc(far_parts, 1)
                nc.vector.tensor_reduce(low_high[:, 1:2], highest[:, :], AX.X, ALU.max).then_inc(far_parts, 1)
                dve.wait_ge(far_parts, 3 * BLOCKS + 2)
                nc.vector.tensor_scalar(far[:, 0:1], low_high[:, 0:1], 0.0, None, ALU.is_lt).then_inc(far_parts, 1)
                dve.wait_ge(far_parts, 3 * BLOCKS + 3)
                nc.vector.scalar_tensor_tensor(far[:, 0:1], low_high[:, 1:2], float(KEYS), far[:, 0:1],
                                               ALU.is_ge, ALU.add).then_inc(far_parts, 1)
                dve.wait_ge(far_parts, 3 * BLOCKS + 4)
                nc.vector.tensor_copy(far[:, 1:2], far[:, 0:1]).then_inc(far_parts, 1)
                dve.wait_ge(far_parts, 3 * BLOCKS + 5)
                dve.wait_ge(base_parts, 3)
                nc.vector.tensor_tensor(far[0:1, 1:2], far[0:1, 1:2], n_misplaced[:, :], ALU.add).then_inc(far_counted, 1)

            def build_onehot(into, g, done):
                kt = key_t[:, bass.ds(g * CH, CH)]
                nc.vector.tensor_tensor(into, p_iota[:, 0:KEYS].unsqueeze(1).to_broadcast([P, CH, KEYS]),
                                        kt.unsqueeze(2).to_broadcast([P, CH, KEYS]), ALU.is_equal).then_inc(done, 1)

            def load_bases(g, n):
                return nc.values_load_multi_w_load_instructions(
                    bases[0:1, bass.ds(g, n)], engines=[dve.engine], min_val=0, max_val=N - 1)[1]

            def bases_of_lot(k, q, first=0, n=LOT):
                of = list(load_bases(k * TURN + (DENSE + q * LOT + first), n))
                if first == 0 and q == 0 and not is0(k):
                    of.insert(DAT, load_bases(k - 1, 1)[0])
                return of

            def add_group(k, q, i, base):
                at = (0 if is0(k) else k * (TURN + 1) - 1 + (q > 0)) + q * LOT + i
                mid = q == 0 and not is0(k)
                column = (LOT if i == DAT else i - (i > DAT)) if mid else i
                if not (is0(k) and at == 0):
                    dve.wait_ge(added, at)
                dve.wait_ge(h_ready, LOTS * k + (q + 1))
                window = acc[:, bass.ds(base, WIN)]
                nc.vector.tensor_tensor(window, window, p_h[q % 2][:, column * WIN:(column + 1) * WIN],
                                        ALU.add).then_inc(added, 1)

            def start_dense(k):
                if follows_dense(k):
                    dve.wait_ge(node1h_ready, (k - 1) * PIECES)
                nc.vector.tensor_tensor(src_rel[:, :, :],
                                        src_t[:, bass.ds(k * CH, CH)].unsqueeze(2).to_broadcast([P, CH, TILES]),
                                        tile_base[:, :].unsqueeze(1).to_broadcast([P, CH, TILES]),
                                        ALU.subtract).then_inc(src_rel_ready, 1)

            def compare_nodes(k, n):
                w = CUTS[n + 1] - CUTS[n]
                if n == 0:
                    dve.wait_ge(src_rel_ready, k)
                if n >= 2:
                    dve.wait_ge(counts_ready, (k - 1) * PAIRS + pairs_through(n - 2))
                elif follows_dense(k):
                    dve.wait_ge(counts_ready, (k - 2) * PAIRS + pairs_through(n + PIECES - 2))
                nc.vector.tensor_tensor(node1h[:, n % 2, :, 0:w, :],
                                        p_iota[:, 0:P].unsqueeze(1).unsqueeze(1).to_broadcast([P, CH, w, P]),
                                        src_rel[:, :, CUTS[n]:CUTS[n + 1]].unsqueeze(3).to_broadcast([P, CH, w, P]),
                                        ALU.is_equal).then_inc(node1h_ready, 1)

            def compare_lot(k, q, dense=True, n=LOT):
                back = None if in_first_lots(k, q) else two_back(k, q)
                of = []
                for i in range(n):
                    s = q * LOT + i
                    if not (is0(k) and q == 0):
                        before = pos(k, s - LOT) if q else pos(k - 1, s + TURN - LOT)
                        dve.wait_ge(z_ready, before + 1)
                    build_onehot((onehot if is_f32(k) else onehot_b)[:, i, :, :], k * TURN + (DENSE + s), onehot_ready)
                    if back and i == 0:
                        of += bases_of_lot(*back, 0, HALF)
                    if back and i == HALF:
                        of += bases_of_lot(*back, HALF, LOT - HALF)
                    if back:
                        add_group(*back, i, of[i])
                    if dense and not is0(k):
                        if s == 0:
                            start_dense(k)
                        compare_nodes(k, s)
                        if s == 0:
                            if follows_dense(k):
                                dve.wait_ge(counts_ready, (k - 1) * PAIRS)
                            build_onehot(onehot_d[:, :, :], k, onehot_d_ready)
                if back:
                    if n <= HALF:
                        of += bases_of_lot(*back, HALF, LOT - HALF)
                    for i in range(n, len(of)):
                        add_group(*back, i, of[i])

            def split():
                for n in range(STEPS + 1):
                    for i in splits_at(n):
                        dve.wait_ge(x_hi, i + 1)
                        dve.wait_ge(x_turned, -(-(i + 1) * ST // PER))
                        piece = x_f[:, i * ST:(i + 1) * ST, :]
                        nc.vector.tensor_tensor(piece, piece, x_parts[:, i * ST:(i + 1) * ST, 0, :],
                                                ALU.subtract).then_inc(x_less_hi, 1)
                    for i in splits_at(n - 1):
                        dve.wait_ge(x_mid, i + 1)
                        nc.vector.tensor_tensor(x_parts[:, i * ST:(i + 1) * ST, 2, :], x_f[:, i * ST:(i + 1) * ST, :],
                                                x_parts[:, i * ST:(i + 1) * ST, 1, :], ALU.subtract).then_inc(x_split, 1)

            dve.wait_ge(turned_out, 2)
            dve.wait_ge(const_in_psum, 1)
            compare_lot(0, 0)
            dve.wait_ge(turned_out, 4 * BLOCKS)
            nc.vector.memset(x_f[:, TILES - 1, :], 0.0).then_inc(x_pad, 1)
            nc.vector.memset(acc[:, TILES * P:ACC], 0.0).then_inc(acc_set, 1)
            dve.wait_ge(bases_in, 32)
            look_for_strays()
            for q in range(1, LOTS):
                compare_lot(0, q)
            build_onehot(onehot_0[:, :, :], 0, onehot_0_ready)
            split()
            dve.wait_ge(acc_set, BATCHES + 1)
            for q in range(LOTS):
                compare_lot(1, q)
            with dve.Fori(2, TURNS) as k:
                for q in range(LOTS):
                    compare_lot(k, q)
            for q, n in enumerate(REST_LOTS):
                compare_lot(TURNS, q, dense=False, n=n)

            def take_stats(n):
                dve.wait_ge(y_ready, n + 1)
                done = tiles_through(n) - len(tiles_of(n))
                for i, t in enumerate(tiles_of(n)):
                    m = min(P, N - t * P)
                    nc.vector.bn_stats(stats[0:m, t, :], p_y[n % 4][0:m, i * D:(i + 1) * D]).then_inc(stats_taken, 1)
                for i, t in enumerate(tiles_of(n)):
                    m = min(P, N - t * P)
                    dve.wait_ge(stats_taken, done + i + 1)
                    nc.vector.bn_aggr(mean_var[0:m, t, :], stats[0:m, t, :]).then_inc(aggregated, 1)

            def finish(n):
                t0, t1 = tiles_of(n)[0], tiles_of(n)[-1] + 1
                m = min(P, N - t0 * P)
                dve.wait_ge(std_known, n + 1)
                nc.vector.reciprocal(rstd[0:m, t0:t1], std[0:m, t0:t1]).then_inc(rstd_known, 1)
                dve.wait_ge(rstd_known, n + 1)
                nc.vector.scalar_tensor_tensor(shift[0:m, t0:t1], mean_var[0:m, t0:t1, 0], -1.0, rstd[0:m, t0:t1],
                                               ALU.mult, ALU.mult).then_inc(norm_known, 1)

            ends = [(TURNS, q) for q in range(len(REST_LOTS))][-2:]
            of_ends = [bases_of_lot(*e, 0, REST_LOTS[e[1]]) for e in ends]
            dve.wait_ge(flag_ready, 1)
            strays = dve.value_load(flag[0:1, 0:1])
            redo = dve.value_load(flag[0:1, 1:2])
            for n in range(EARLY):
                take_stats(n)
                if n >= 1:
                    finish(n - 1)
            finish(EARLY - 1)
            for i, base in enumerate(of_ends[0]):
                add_group(*ends[0], i, base)
            for n in range(EARLY, REDO):
                take_stats(n)
            for i, base in enumerate(of_ends[1]):
                add_group(*ends[1], i, base)
            for n in range(EARLY, REDO):
                finish(n)

            dve.wait_ge(added, GROUPS)
            with dve.If(strays > 0):
                for i in range(4):
                    dve.wait_ge(stored[i], 16 * n_stores(i, REDO))
                nc.vector.tensor_scalar(outside, key_t[:, :], 0.0, None, ALU.is_lt).then_inc(st_keyed, 1)
                nc.vector.tensor_scalar(stray, typ_t[:, :], float(P), pid1[:, 0:1], ALU.mult, ALU.add).then_inc(st_keyed, 1)
                dve.wait_ge(st_keyed, 2)
                nc.vector.scalar_tensor_tensor(outside, key_t[:, :], float(KEYS), outside,
                                               ALU.is_ge, ALU.add).then_inc(st_keyed, 1)
                dve.wait_ge(st_keyed, 3)
                nc.vector.tensor_tensor(stray, stray, outside, ALU.mult).then_inc(st_keyed, 1)
                dve.wait_ge(st_keyed, 4)
                nc.vector.tensor_scalar(stray, stray, -1.0, None, ALU.add).then_inc(st_keyed, 1)
                dve.wait_ge(st_keyed, 5)

                def stray_group(g):
                    first = isinstance(g, int)
                    for j in range(CH):
                        if not (first and j == 0):
                            dve.wait_ge(st_z_ready, g * CH + j)
                        nc.vector.tensor_tensor(st_key1h, iota[:, :],
                                                stray[:, bass.ds(g * CH + j, 1)].to_broadcast([P, R * P]),
                                                ALU.is_equal).then_inc(st_onehot, 1)
                    if not first:
                        dve.wait_ge(st_added, g * NODE_WINS)
                        dve.wait_ge(st_dstep, g * NODE_WINS)
                    nc.vector.tensor_copy(st_dst[:, :], dst_t[:, bass.ds(g * CH, CH)]).then_inc(st_keyed, 1)
                    with dve.Fori(0, NODE_WINS) as w:
                        n = g * NODE_WINS + w
                        dve.wait_ge(st_keyed, g + 6)
                        nc.vector.tensor_tensor(st_dst1h,
                                                iota[:, 0:BANK].unsqueeze(1).to_broadcast([P, CH, BANK]),
                                                st_dst[:, :].unsqueeze(2).to_broadcast([P, CH, BANK]),
                                                ALU.is_equal).then_inc(st_win, 1)
                        dve.wait_ge(st_win, n + 1)
                        nc.vector.tensor_scalar(st_dst[:, :], st_dst[:, :], float(-BANK), None,
                                                ALU.add).then_inc(st_dstep, 1)
                        dve.wait_ge(st_dstep, n + 1)
                        dve.wait_ge(st_sum, n + 1)
                        nodes = acc[:, bass.ds(w * BANK, BANK)]
                        nc.vector.tensor_tensor(nodes, nodes, p_z[1][:, :], ALU.add).then_inc(st_added, 1)

                stray_group(0)
                with dve.Fori(1, GROUPS) as g:
                    stray_group(g)
                dve.wait_ge(st_added, GROUPS * NODE_WINS)

            for n in range(REDO, BATCHES):
                take_stats(n)
                if n > REDO:
                    finish(n - 1)
            finish(BATCHES - 1)
            with dve.If(redo > 0):
                dve.wait_ge(aggregated, TILES)
                dve.wait_ge(norm_known, BATCHES)
                dve.wait_ge(normed, TILES)
                for n in range(BATCHES, BATCHES + REDO):
                    take_stats(n)
                    finish(n)

        @block.tensor
        def _(pe):
            pe.wait_ge(ident_ready, 1)
            for b in range(BLOCKS):
                for q, listed in enumerate((src_f, key_f, typ_f, dst_f)):
                    n = 4 * b + q
                    if q == 0:
                        pe.wait_ge(src_cast, b + 1)
                    if q == 1:
                        pe.wait_ge(keyed, b + 1)
                    if n >= 2:
                        pe.wait_ge(turned_out, n - 1)
                    for j in range(CH):
                        last = nc.tensor.transpose(p_turn[n % 2][:, j * P:(j + 1) * P], listed[:, b, j:GE:CH],
                                                   ident[:, :])
                    last.then_inc(turned, 1)

            def add_up(terms, z):
                for n, (lhs, rhs) in enumerate(terms):
                    last = nc.tensor.matmul(z, lhs, rhs, start=(n == 0), stop=(n == len(terms) - 1))
                last.then_inc(z_ready, 1)

            def sums(k, s):
                pe.wait_ge(landed[s % SLOTS], (k * 2 + (s // SLOTS + 1)) * (16 * CH))
                pe.wait_ge(onehot_ready, k * TURN + (s + 1))
                if not (is0(k) and s < 2):
                    pe.wait_ge(z_copied, (pos(k, s - 2) if s >= 2 else pos(k - 1, s + TURN - 2)) + 1)
                slot, i = s % SLOTS, s % LOT
                if is_f32(k):
                    terms = [(rows[:, slot, j, :], onehot[:, i, j, :]) for j in range(CH)]
                else:
                    terms = [(rows_b[:, slot, j, a * D:(a + 1) * D], onehot_b[:, i, j, :])
                             for j in range(CH) for a in range(PARTS)]
                add_up(terms, p_z[s % 2][:, 0:KEYS])

            def sums_0():
                pe.wait_ge(landed_0, 16 * CH)
                pe.wait_ge(onehot_0_ready, 1)
                add_up([(rows_0[:, j, :], onehot_0[:, j, :]) for j in range(CH)], p_zd)

            def count(k, n, c):
                if c == 0:
                    pe.wait_ge(onehot_d_ready, k)
                if c == pairs_of(n)[0]:
                    pe.wait_ge(node1h_ready, (k - 1) * PIECES + (n + 1))
                if c >= 2 or follows_dense(k):
                    pe.wait_ge(counts_copied, (k - 1) * PAIRS + max(0, c - 1))
                for i, t in enumerate(range(2 * c, min(TILES, 2 * c + 2))):
                    for j in range(CH):
                        last = nc.tensor.matmul(p_turn[c % 2][:, i * KEYS:(i + 1) * KEYS], node1h[:, n % 2, j, t - CUTS[n], :],
                                                onehot_d[:, j, :], start=(j == 0), stop=(j == CH - 1))
                last.then_inc(counts_ready, 1)

            def weigh(k, c):
                pe.wait_ge(counts_copied, (k - 1) * PAIRS + (c + 1))
                if c == 0:
                    pe.wait_ge(z_copied, pos_d(k) + 1)
                for i, t in enumerate(range(2 * c, min(TILES, 2 * c + 2))):
                    for a in range(PARTS):
                        last = nc.tensor.matmul(p_zd, x_parts[:, t, a, :], counts[:, c % 2, i * KEYS:(i + 1) * KEYS],
                                                start=(t == 0 and a == 0), stop=(t == TILES - 1 and a == PARTS - 1))
                if c == PAIRS - 1:
                    last.then_inc(z_ready, 1)

            def products(k, q, n=LOT):
                with_dense = q == 0 and not is0(k)
                pe.wait_ge(z_copied, through(k, q, n))
                if not in_first_lots(k, q):
                    pe.wait_ge(added, through(*two_back(k, q)))
                m = LOT + 1 if with_dense else n
                for r in range(R):
                    last = nc.tensor.matmul(p_h[q % 2][:, 0:m * WIN], W_sb[:, r, :],
                                            z_sb[:, q % 2, r, 0:m, :].rearrange("p i d -> p (i d)"),
                                            start=(r == 0), stop=(r == R - 1))
                last.then_inc(h_ready, 1)

            def turn_x(s):
                for b in batches_at(s - LOT):
                    pe.wait_ge(x_in, 32)
                    pe.wait_ge(turned_out, 4 * BLOCKS)
                    if b >= 2:
                        pe.wait_ge(acc_set, b)
                    for i in range(min(PER, TILES - b * PER)):
                        last = nc.tensor.transpose(p_turn[b % 2][:, i * P:(i + 1) * P], x_f[:, b * PER + i, :], ident[:, :])
                    last.then_inc(x_turned, 1)

            def turn(k, sizes=(LOT,) * LOTS, dense=True, after=None):
                for q, n in enumerate(sizes):
                    for s in range(q * LOT, q * LOT + n):
                        if s == q * LOT + 1 and not (is0(k) and q == 0):
                            products(*((k, q - 1) if q else (k - 1, LOTS - 1)))
                        sums(k, s)
                        if is0(k):
                            turn_x(s)
                            continue
                        if s == DAT - 1:
                            if follows_dense(k):
                                weigh(k - 1, PAIRS - 1)
                            else:
                                sums_0()
                        if dense:
                            for c in pairs_of(s):
                                count(k, s, c)
                                if c >= 1:
                                    weigh(k, c - 1)
                        if after and early_at(s):
                            after(s)
                    if n == 1 and q:
                        products(k, q - 1)

            pe.wait_ge(w_in, 16)
            turn(0)
            pe.wait_ge(far_counted, 1)
            pe.wait_ge(acc_set, BATCHES + 1)
            nc.tensor.matmul(p_flag, ones[:, :], far[:, :], start=True, stop=True).then_inc(far_summed, 1)
            pe.wait_ge(flag_ready, 1)
            pe.wait_ge(x_split, SPLITS)
            turn(1)
            with pe.Fori(2, TURNS) as k:
                turn(k)
            strays = pe.value_load(flag[0:1, 0:1])
            redo = pe.value_load(flag[0:1, 1:2])

            def turn_y(n):
                if n >= 4:
                    pe.wait_ge(normed, tiles_through(n - 4))
                for i, t in enumerate(tiles_of(n)):
                    m = min(P, N - t * P)
                    last = nc.tensor.transpose(p_y[n % 4][0:m, i * D:(i + 1) * D], acc[:, t * P:t * P + m], ident[:, :])
                last.then_inc(y_ready, 1)

            def turn_early(s):
                pe.wait_ge(added, through(TURNS - 1, LOTS - 1))
                pe.wait_ge(z_copied, pos_d(TURNS) + 1)
                pe.wait_ge(onehot_ready, GATHERED)
                for n in early_at(s):
                    turn_y(n)

            turn(TURNS, sizes=REST_LOTS, dense=False, after=turn_early)
            pe.wait_ge(added, through(TURNS, len(REST_LOTS) - 2))
            for n in range(EARLY, REDO):
                turn_y(n)
            products(TURNS, len(REST_LOTS) - 1, REST_LOTS[-1])

            with pe.If(strays > 0):
                pe.wait_ge(normed, tiles_through(REDO - 1))
                def stray_group(g):
                    pe.wait_ge(st_landed, (g + 1) * (16 * CH))
                    for j in range(CH):
                        pe.wait_ge(st_onehot, g * CH + (j + 1))
                        for h in range(2):
                            last = nc.tensor.matmul(p_turn[h][:, :], rows[:, 0, j, :], st_key1h[:, h * BANK:(h + 1) * BANK],
                                                    start=True, stop=True)
                        last.then_inc(st_z_ready, 1)
                        pe.wait_ge(st_z_copied, g * CH + (j + 1))
                        if j >= 1:
                            pe.wait_ge(st_m_copied, g * CH + j)
                        for r in range(R):
                            last = nc.tensor.matmul(p_z[0][:, 0:D], st_z[:, r, :], W_sb[:, r, :],
                                                    start=(r == 0), stop=(r == R - 1))
                        last.then_inc(st_m_ready, 1)
                    with pe.Fori(0, NODE_WINS) as w:
                        pe.wait_ge(st_m_copied, (g + 1) * CH)
                        pe.wait_ge(st_win, g * NODE_WINS + w + 1)
                        for j in range(CH):
                            last = nc.tensor.matmul(p_z[1][:, :], st_msg[:, j, :], st_dst1h[:, j, :],
                                                    start=(j == 0), stop=(j == CH - 1))
                        last.then_inc(st_sum, 1)

                stray_group(0)
                with pe.Fori(1, GROUPS) as g:
                    stray_group(g)
                pe.wait_ge(st_added, GROUPS * NODE_WINS)

            pe.wait_ge(added, GROUPS)
            for n in range(REDO, BATCHES):
                turn_y(n)
            with pe.If(redo > 0):
                for n in range(BATCHES, BATCHES + REDO):
                    turn_y(n)


def kernel(x, src, dst, edge_type_8, L0_gnn_W):
    import numpy as np
    import concourse.bacc as bacc
    from concourse.bass_utils import run_bass_kernel_spmd

    nc = bacc.Bacc("TRN2", target_bir_lowering=False, num_devices=1)
    arrays, args = {}, []
    for name, a in (("x", x), ("src", src), ("dst", dst), ("edge_type", edge_type_8), ("W", L0_gnn_W)):
        a = np.ascontiguousarray(a)
        arrays[f"in_{name}"] = a
        args.append(nc.dram_tensor(f"in_{name}", a.shape, mybir.dt.from_np(a.dtype), kind="ExternalInput").ap())
    args.append(nc.dram_tensor("out_0", arrays["in_x"].shape, FP32, kind="ExternalOutput").ap())
    build(nc, *args)
    return run_bass_kernel_spmd(nc, [arrays], core_ids=[0]).results[0]["out_0"]
```
